# Optimizing a Trainium2 kernel written in Bass

```python
import numpy as np
import jax
import jax.numpy as jnp

def _softmax(x, axis=-1):
    return jax.nn.softmax(x, axis=axis)

def _gelu(x):
    return jax.nn.gelu(x, approximate=True)

def _silu(x):
    return jax.nn.silu(x)

def _sigmoid(x):
    return jax.nn.sigmoid(x)

def _layernorm(x, axis=-1, eps=1e-05):
    m = jnp.mean(x, axis=axis, keepdims=True)
    v = jnp.var(x, axis=axis, keepdims=True)
    return (x - m) / jnp.sqrt(v + eps)

def _scatter_add(tgt, idx, src, axis=0):
    return tgt.at[idx].add(src)

def _segment_sum(src, seg, n):
    return jax.ops.segment_sum(src, seg, n)
kernel_name = 'mk_conv_preact_d4_conv_nchw8_r4_8d78a8'

def setup_inputs(seed: int=0):
    np.random.seed(seed)
    _w = jnp.asarray

    def _rec_inputs():
        import jax
        import jax.numpy as jnp
        _gk = jax.random.key(seed)
        x = -0.0001546 + 1 * jax.random.normal(jax.random.fold_in(_gk, 1), (4, 8, 256, 256), jnp.float32)
        return x
    x = _rec_inputs()

    def _L0_conv_setup():
        import jax, jax.numpy as jnp
        import numpy as np
        key = jax.random.key(seed)
        k1, k2, k3 = jax.random.split(key, 3)
        x = jax.random.normal(k1, (16, 8, 256, 256), dtype=jnp.float32)
        weight = jax.random.normal(k2, (8, 8, 3, 3), dtype=jnp.float32) * 0.1
        bias = jax.random.normal(k3, (8,), dtype=jnp.float32) * 0.1
        return {'x': x, 'weight': weight, 'bias': bias}
    _L0_conv_all = _L0_conv_setup()
    _L0_conv_in = {k: v for k, v in _L0_conv_all.items() if k in ('weight', 'bias')}
    del _L0_conv_all

    def _L1_conv_setup():
        import jax, jax.numpy as jnp
        import numpy as np
        key = jax.random.key(seed)
        k1, k2, k3 = jax.random.split(key, 3)
        x = jax.random.normal(k1, (16, 8, 256, 256), dtype=jnp.float32)
        weight = jax.random.normal(k2, (8, 8, 3, 3), dtype=jnp.float32) * 0.1
        bias = jax.random.normal(k3, (8,), dtype=jnp.float32) * 0.1
        return {'x': x, 'weight': weight, 'bias': bias}
    _L1_conv_all = _L1_conv_setup()
    _L1_conv_in = {k: v for k, v in _L1_conv_all.items() if k in ('weight', 'bias')}
    del _L1_conv_all

    def _L2_conv_setup():
        import jax, jax.numpy as jnp
        import numpy as np
        B, E, N, D, F = (2, 8, 256, 256, 1024)
        key = jax.random.key(seed)
        k_x, k_w1, k_w2 = jax.random.split(key, 3)
        x = jax.random.normal(k_x, (B, E, N, D), dtype=jnp.float32)
        w1 = jax.random.normal(k_w1, (E, D, F), dtype=jnp.float32) * (1.0 / np.sqrt(D))
        b1 = jnp.zeros((E, F), dtype=jnp.float32)
        w2 = jax.random.normal(k_w2, (E, F, D), dtype=jnp.float32) * (1.0 / np.sqrt(F))
        b2 = jnp.zeros((E, D), dtype=jnp.float32)
        return {'x': x, 'w1': w1, 'b1': b1, 'w2': w2, 'b2': b2}
    _L2_conv_all = _L2_conv_setup()
    _L2_conv_in = {k: v for k, v in _L2_conv_all.items() if k in ('w1', 'b1', 'w2', 'b2')}
    del _L2_conv_all

    def _L3_conv_setup():
        import jax, jax.numpy as jnp
        import numpy as np
        key = jax.random.key(seed)
        k1, k2, k3 = jax.random.split(key, 3)
        x = jax.random.normal(k1, (16, 8, 256, 256), dtype=jnp.float32)
        weight = jax.random.normal(k2, (8, 8, 3, 3), dtype=jnp.float32) * 0.1
        bias = jax.random.normal(k3, (8,), dtype=jnp.float32) * 0.1
        return {'x': x, 'weight': weight, 'bias': bias}
    _L3_conv_all = _L3_conv_setup()
    _L3_conv_in = {k: v for k, v in _L3_conv_all.items() if k in ('weight', 'bias')}
    del _L3_conv_all
    return {'x': x, 'L0_conv_weight': _L0_conv_in['weight'], 'L0_conv_bias': _L0_conv_in['bias'], 'L1_conv_weight': _L1_conv_in['weight'], 'L1_conv_bias': _L1_conv_in['bias'], 'L2_conv_w1': _L2_conv_in['w1'], 'L2_conv_b1': _L2_conv_in['b1'], 'L2_conv_w2': _L2_conv_in['w2'], 'L2_conv_b2': _L2_conv_in['b2'], 'L3_conv_weight': _L3_conv_in['weight'], 'L3_conv_bias': _L3_conv_in['bias']}

def reference(x, L0_conv_weight, L0_conv_bias, L1_conv_weight, L1_conv_bias, L2_conv_w1, L2_conv_b1, L2_conv_w2, L2_conv_b2, L3_conv_weight, L3_conv_bias):
    import jax
    import jax.numpy as jnp

    def _L0_conv_ref(x, weight, bias):
        import jax, jax.numpy as jnp
        import numpy as np
        out = jax.lax.conv_general_dilated(x, weight, window_strides=(1, 1), padding=((1, 1), (1, 1)), dimension_numbers=('NCHW', 'OIHW', 'NCHW'))
        return out + bias[None, :, None, None]

    def _L1_conv_ref(x, weight, bias):
        import jax, jax.numpy as jnp
        import numpy as np
        out = jax.lax.conv_general_dilated(x, weight, window_strides=(1, 1), padding=((1, 1), (1, 1)), dimension_numbers=('NCHW', 'OIHW', 'NCHW'))
        return out + bias[None, :, None, None]

    def _L2_conv_ref(x, w1, b1, w2, b2):
        import jax, jax.numpy as jnp
        import numpy as np
        B, E, N, D, F = (2, 8, 256, 256, 1024)
        h = jnp.einsum('bend,edf->benf', x, w1) + b1[None, :, None, :]
        h = jax.nn.gelu(h, approximate=False)
        out = jnp.einsum('benf,efd->bend', h, w2) + b2[None, :, None, :]
        return out

    def _L3_conv_ref(x, weight, bias):
        import jax, jax.numpy as jnp
        import numpy as np
        out = jax.lax.conv_general_dilated(x, weight, window_strides=(1, 1), padding=((1, 1), (1, 1)), dimension_numbers=('NCHW', 'OIHW', 'NCHW'))
        return out + bias[None, :, None, None]

    def _gn(v, G=4, eps=1e-05):
        B_, C_, H_, W_ = v.shape
        g = v.reshape(B_, G, C_ // G, H_, W_)
        m = jnp.mean(g, axis=(2, 3, 4), keepdims=True)
        s = jnp.var(g, axis=(2, 3, 4), keepdims=True)
        return ((g - m) / jnp.sqrt(s + eps)).reshape(v.shape)

    def _ln_c(v, eps=1e-06):
        m = jnp.mean(v, axis=1, keepdims=True)
        s = jnp.var(v, axis=1, keepdims=True)
        return (v - m) / jnp.sqrt(s + eps)

    def _ln_t(v, eps=1e-05):
        m = jnp.mean(v, axis=-1, keepdims=True)
        s = jnp.var(v, axis=-1, keepdims=True)
        return (v - m) / jnp.sqrt(s + eps)

    def _to_tokens(v):
        B_, C_, H_, W_ = v.shape
        return v.reshape(B_, C_, H_ * W_).transpose(0, 2, 1)

    def _from_tokens(t, like):
        B_, C_, H_, W_ = like.shape
        return t.transpose(0, 2, 1).reshape(B_, C_, H_, W_)
    x = x + _L0_conv_ref(_gn(x), L0_conv_weight, L0_conv_bias)
    x = x + _L1_conv_ref(_gn(x), L1_conv_weight, L1_conv_bias)
    x = x + _L2_conv_ref(_gn(x), L2_conv_w1, L2_conv_b1, L2_conv_w2, L2_conv_b2)
    x = x + _L3_conv_ref(_gn(x), L3_conv_weight, L3_conv_bias)
    return x

_drawn_inputs = setup_inputs


def setup_inputs(seed=0):
    import zlib

    import numpy as np

    out = dict(_drawn_inputs(seed))
    spreads = {'L2_conv_b1': (0.0, 0.284), 'L2_conv_b2': (0.0, 0.1)}
    factors = {}
    for name, (base, spread) in spreads.items():
        noise = np.random.default_rng([zlib.crc32(name.encode()), seed]).standard_normal(out[name].shape)
        drawn = base * np.exp(spread * noise) if base else spread * noise
        out[name] = jnp.asarray(drawn.astype(out[name].dtype))
    for name, factor in factors.items():
        out[name] = (out[name] * factor).astype(out[name].dtype)
    return out
```

```python
from contextlib import ExitStack

import concourse.bass as bass
from concourse import mybir

ALU = mybir.AluOpType
ACT = mybir.ActivationFunctionType
F32 = mybir.dt.float32
F16 = mybir.dt.float16
U32 = mybir.dt.uint32
AX_X = mybir.AxisListType.X
ds = bass.ds

P = 128
NB, NC, NH, NW = 4, 8, 256, 256
R = P // NC
NT = NH // R
IMG = NT * NW
CH = 512
NCH = IMG // CH
TC = CH // NW
PITCH = NW + 2
GROUP = 2 * R
EPS = 1e-5
NE, NF = 8, 1024
FT = NF // P
DH = NW // P
NPAIR = NB // 2
TT = 2 * NT
KX = KY = 3
HROWS = 2 * NC * KX
ONES = 2 * HROWS
KH = ONES + 1
XS, WS, HS = 64.0, 256.0, 16.0

FINISH = {0: [2], 1: [3], 2: [4, 5], 3: [6], 4: [7], 5: [8], 6: [9], 7: [10],
          8: [13], 9: [14], 10: [15], 11: []}


def stat_of_step(g):
    return g if g < 8 else g + 4


def image_of_step(g):
    return g % 4


def one(i):
    return i


RSTD_STEPS = 5
CW_DMAS = 13


def bass_program(nc, x, cw, cb, w1, b1, w2, b2, out):
    ctx = ExitStack()

    def at(name, offset, shape, dt):
        return nc.alloc_sbuf_tensor_at(name, shape, dt, offset=offset)

    def sem(name):
        return nc.alloc_semaphore(name)

    base = (nc.sbuf_base + 31) // 32 * 32
    X_OFF = base
    XY_OFF = X_OFF + NB * IMG * 4
    XN_OFF = XY_OFF + NB * IMG * 4
    XN_SLOT = 2 * NT * PITCH * 2
    HALO_OFF = XN_OFF + 2 * XN_SLOT
    HALO_SLOT = NT * PITCH * 2
    W1S_OFF = HALO_OFF + 2 * HALO_SLOT
    W2S_OFF = W1S_OFF + 2 * DH * NF * 2
    CW_OFF = W2S_OFF + 2 * FT * NW * 2
    SCR_OFF = CW_OFF + 3 * 11 * P * 2
    C_OFF = SCR_OFF + 2 * CH * 4

    X = at("X", X_OFF, [P, NB * IMG], F32)
    XT = at("XT", XY_OFF, [P, NPAIR, DH, TT, NC, 2, R], F16)
    YT = at("YT", XY_OFF, [P, NPAIR, DH, TT, NC * R], F32)
    XN = [at(f"XN{s}", XN_OFF + s * XN_SLOT, [P, 2, NT, PITCH], F16) for s in range(2)]
    HALO = [at(f"HALO{s}", HALO_OFF + s * HALO_SLOT, [P, NT, PITCH], F16) for s in range(2)]
    HID = [at(f"HID{p}", XN_OFF + p * XN_SLOT, [P, 2, FT, CH], F16) for p in range(NPAIR)]
    W1F = at("W1F", HALO_OFF, [P, DH * NF], F32)
    W2F = at("W2F", HALO_OFF + HALO_SLOT, [P, FT * NW], F32)
    W1S = at("W1S", W1S_OFF, [P, 2, DH * NF], F16)
    W2S = at("W2S", W2S_OFF, [P, 2, FT * NW], F16)
    PRE = at("PRE", W2S_OFF, [P, 4, CH], F32)
    CWT = at("CWT", CW_OFF, [P, 3, 8, P], F16)
    SCR = at("SCR", SCR_OFF, [P, 2, CH], F32)
    o = C_OFF
    IDF = at("IDF", o, [P, P], F32); o += P * 4
    GRP = at("GRP", o, [P, P], F32); o += P * 4
    BT = at("BT", o, [P, (FT + DH) * NE], F32); o += (FT + DH) * NE * 4
    ST = at("ST", o, [P, 2, NCH, 6], F32); o += 2 * NCH * 6 * 4
    MV = at("MV", o, [P, 16, 2], F32); o += 16 * 2 * 4
    SM = at("SM", o, [P, 16, 4], F32); o += 16 * 4 * 4
    SC = at("SC", o, [P, 16, 2], F32); o += 16 * 2 * 4
    RS = at("RS", o, [P, 8], F32); o += 32
    HALF = RS[:, 2:3]
    assert o <= nc.sbuf_usable_end, (o, nc.sbuf_usable_end)
    s0 = XY_OFF
    TW = at("TW", s0, [P, 3, KX, KY, NC], F32); s0 += 3 * NC * 9 * 4
    HW_ = at("HW_", s0, [P, 3, NC, R], F32); s0 += 3 * P * 4
    MSK = at("MSK", s0, [P, KY, R], F32); s0 += KY * R * 4
    BLK = at("BLK", s0, [P, NC, R], F32); s0 += P * 4
    SEL = at("SEL", s0, [P, KY, NC, R], F32); s0 += KY * P * 4
    ACC = at("ACC", s0, [P, 3, KX, NC, R], F32); s0 += 3 * KX * P * 4
    TMP = at("TMP", s0, [P, 3, KX, NC, R], F32); s0 += 3 * KX * P * 4
    BR = at("BR", s0, [P, 3, NC], F32); s0 += 3 * NC * 4
    HTM = at("HTM", s0, [P, 3, P], F32); s0 += 3 * P * 4
    BB = at("BB", s0, [(FT + DH) * NE, P], F32)

    PS = nc.alloc_psum_tensor("PS", [P, 8 * CH], F32)
    RING, G2_BANK, TR_BANK = 4, 4, 6

    def bank(k):
        return PS[:, ds(k * CH, CH)] if not isinstance(k, int) else PS[:, k * CH:(k + 1) * CH]

    def stat_psum(n, col):
        k = 0 if n == 12 else 5
        return PS[:, k * CH + col:k * CH + col + 1]

    def tr_bank(m):
        return bank(TR_BANK + m % 2).rearrange("p (h t c r) -> p h (t c) r", h=DH, t=TC, c=NC)

    def xt_part(b, j, h):
        tt = (b % 2) * NT + j * TC
        return XT[:, b // 2, :, tt:tt + TC, :, h, :].rearrange("p h t c r -> p h (t c) r")

    def yt_part(e, p, dh):
        return YT[:, p, dh, :, ds(e * R, R)]

    x_in = [sem(f"x_in{i}") for i in range(NB + 1)]
    cw_in = [sem(f"cw_in{l}") for l in range(3)]
    bb_in = sem("bb_in")
    halo_in = [sem(f"halo_in{s}") for s in range(2)]
    w1_in, w2_in = sem("w1_in"), sem("w2_in")
    out_done = sem("out_done")
    const_ok = sem("const_ok")
    msk_ok = sem("msk_ok")
    hw_zero = sem("hw_zero")
    cwt_zero = sem("cwt_zero")
    pads_ok = [sem(f"pads_ok{s}") for s in range(2)]
    halo_ok = [sem(f"halo_ok{s}") for s in range(2)]
    red_ok = sem("red_ok")
    build_ok = [sem(f"build_ok{l}") for l in range(3)]
    bt_mm, bt_ok = sem("bt_mm"), sem("bt_ok")
    bn_ok = sem("bn_ok")
    mv_ok = sem("mv_ok")
    mean_mm = sem("mean_mm")
    dev_ok = sem("dev_ok")
    spread_ok = sem("spread_ok")
    var_mm = sem("var_mm")
    var_ok = sem("var_ok")
    rstd_ok = sem("rstd_ok")
    half_ok = sem("half_ok")
    norm_ok = sem("norm_ok")
    xn_ok = sem("xn_ok")
    hi_ok = sem("hi_ok")
    lo_ok = sem("lo_ok")
    conv_mm = sem("conv_mm")
    x_new = sem("x_new")
    pre_ok = sem("pre_ok")
    pre_mm = sem("pre_mm")
    xt_hi = sem("xt_hi")
    xt_lo = sem("xt_lo")
    w1_hi, w1_ok = sem("w1_hi"), sem("w1_ok")
    w2_hi, w2_ok = sem("w2_hi"), sem("w2_ok")
    g1_mm = sem("g1_mm")
    gelu_ok = sem("gelu_ok")
    hid_hi, hid_ok = sem("hid_hi"), sem("hid_ok")
    g2_mm = sem("g2_mm")
    yt_ok = sem("yt_ok")
    ty_mm = sem("ty_mm")

    block = ctx.enter_context(nc.Block())

    order = [("c", g, i) for g in range(8) for i in range(NCH)]
    order += [("y", b, i) for b in range(2) for i in range(NCH)]
    for g in (8, 9):
        for i in range(NCH):
            order += [("y", g - 6, i), ("c", g, i)]
    order += [("c", g, i) for g in (10, 11) for i in range(NCH)]
    x_new_at = {k: n + 1 for n, k in enumerate(order)}

    def last_x_new(key):
        return x_new_at[(key[0], key[1], NCH - 1)]

    @block.sync
    def _(sp):
        def move_image(b, t0, t1, store, signal):
            for c in range(NC):
                sb = X[c * R:(c + 1) * R, b * IMG + t0 * NW:b * IMG + t1 * NW]
                sb = sb.rearrange("r (t w) -> r t w", w=NW)
                dr = (out if store else x)[b, c].rearrange("(t r) w -> r t w", r=R)[:, t0:t1]
                sp.dma_start(dr if store else sb, sb if store else dr).then_inc(signal, 16)

        move_image(0, 0, NT // 2, False, x_in[0])
        move_image(0, NT // 2, NT, False, x_in[1])
        for b in range(1, NB):
            move_image(b, 0, NT, False, x_in[b + 1])

        run = (NT - 2) * PITCH + NW

        def halos(g):
            s = g % 2
            if g >= 2:
                sp.wait_ge(conv_mm, NCH * (g - 1))
            sp.wait_ge(pads_ok[s], 1 if g < 8 else 2)
            sp.wait_ge(halo_ok[s], 2 if g < 8 else 4)
            dst = HALO[s][:].rearrange("p t w -> p (t w)")
            for h in range(2):
                sp.wait_ge(hi_ok if h == 0 else lo_ok, NCH * (g + 1))
                for side in range(2):
                    src = XN[s][(R - 1) * (1 - side):P:R, h, side:]
                    src = src.rearrange("p t w -> p (t w)")
                    src = bass.AP(src.tensor, src.offset, [src.ap[0], (1, KX), (1, run)])
                    row = h * HROWS + side * NC * KX
                    start = (1 - side) * PITCH
                    sp.dma_start(dst[row:row + NC * KX, start:start + run], src
                                 ).then_inc(halo_in[s], 16)

        def load_w1(e):
            if e > 0:
                sp.wait_ge(w1_ok, e)
            sp.dma_start(W1F[:].rearrange("p (h f) -> p h f", h=DH),
                         w1[e].rearrange("(h p) f -> p h f", p=P)).then_inc(w1_in, 16)

        def load_w2(e):
            if e > 0:
                sp.wait_ge(w2_ok, e)
            sp.dma_start(W2F[:].rearrange("p (h d) -> p h d", h=FT),
                         w2[e].rearrange("(h p) d -> p h d", p=P)).then_inc(w2_in, 16)

        for g in range(8):
            halos(g)
        sp.wait_ge(conv_mm, NCH * 7)
        load_w1(0)
        sp.wait_ge(conv_mm, NCH * 8)
        load_w2(0)
        for e in range(1, NE):
            load_w1(e)
            load_w2(e)
        for g in range(8, 12):
            halos(g)
            if g >= 9:
                sp.wait_ge(x_new, last_x_new(("c", g - 1)))
                move_image(g - 9, 0, NT, True, out_done)
        for h in range(2):
            sp.wait_ge(x_new, x_new_at[("c", 11, NCH // 2 * (h + 1) - 1)])
            move_image(3, h * NT // 2, (h + 1) * NT // 2, True, out_done)
        sp.wait_ge(out_done, 16 * NC * (NB + 1))

    BUILD_STEPS = 13

    def build_matrices(eng, l):
        done = [0]

        def step(ins):
            done[0] += 1
            ins.then_inc(build_ok[l], 1)
            eng.wait_ge(build_ok[l], done[0])

        for ky in range(KY):
            weight = TW[:, l, :, ky].unsqueeze(3).broadcast_to([P, KX, NC, R])
            mask = MSK[:, ky].unsqueeze(1).unsqueeze(1).broadcast_to([P, KX, NC, R])
            into = ACC if ky == 0 else TMP
            step(eng.tensor_tensor(into[:, l], weight, mask, ALU.mult))
            if ky >= 1:
                step(eng.tensor_tensor(ACC[:, l], ACC[:, l], TMP[:, l], ALU.add))
        acc = ACC[:, l].rearrange("p k c r -> p (k c r)")
        tmp = TMP[:, l].rearrange("p k c r -> p (k c r)")
        hi = CWT[:, l, 0:3].rearrange("p k m -> p (k m)")
        lo = CWT[:, l, 3:6].rearrange("p k m -> p (k m)")
        step(eng.tensor_copy(HW_[ONES:KH, l],
                             BR[ONES:KH, l].unsqueeze(2).broadcast_to([1, NC, R])))
        step(eng.tensor_scalar(hi, acc, WS, None, ALU.mult))
        step(eng.tensor_scalar(tmp, acc, WS, None, ALU.mult))
        hw = HW_[0:KH, l].rearrange("p c r -> p (c r)")
        step(eng.tensor_scalar(CWT[0:KH, l, 6], hw, WS, None, ALU.mult))
        step(eng.tensor_scalar(HTM[0:KH, l], hw, WS, None, ALU.mult))
        step(eng.tensor_tensor(lo, tmp, hi, ALU.subtract))
        for r0, r1 in ((0, HROWS), (ONES, KH)):
            step(eng.tensor_tensor(CWT[r0:r1, l, 7], HTM[r0:r1, l], CWT[r0:r1, l, 6],
                                   ALU.subtract))


    @block.gpsimd
    def _(pool):
        pool.memset(HALF, -0.5).then_inc(half_ok, 1)
        pool.memset(IDF[:], 0.0).then_inc(const_ok, 1)
        pool.memset(GRP[:], 1.0 / GROUP).then_inc(const_ok, 1)
        pool.memset(BLK[:], 1.0).then_inc(const_ok, 1)
        pool.wait_ge(const_ok, 3)
        blk = BLK[:]
        pool.affine_select(out=blk, in_=blk, compare_op=ALU.is_ge, fill=0.0, base=0,
                           pattern=[[-R, NC], [0, R]], channel_multiplier=1).then_inc(const_ok, 1)
        pool.wait_ge(const_ok, 4)
        pool.affine_select(out=blk, in_=blk, compare_op=ALU.is_ge, fill=0.0, base=R - 1,
                           pattern=[[R, NC], [0, R]], channel_multiplier=-1).then_inc(const_ok, 1)
        pool.wait_ge(const_ok, 5)
        for ky in range(KY):
            pool.affine_select(out=SEL[:, ky], in_=blk, compare_op=ALU.is_equal, fill=0.0,
                               base=1 - ky, pattern=[[-R, NC], [-1, R]],
                               channel_multiplier=1).then_inc(const_ok, 1)
        grp = GRP[:].rearrange("p (g k) -> p g k", k=GROUP)
        pool.affine_select(out=grp, in_=grp, compare_op=ALU.is_ge, fill=0.0, base=0,
                           pattern=[[-GROUP, P // GROUP], [0, GROUP]],
                           channel_multiplier=1).then_inc(const_ok, 1)
        pool.affine_select(out=IDF[:], in_=IDF[:], compare_op=ALU.not_equal, fill=1.0, base=0,
                           pattern=[[-1, P]], channel_multiplier=1).then_inc(const_ok, 1)
        pool.wait_ge(const_ok, 10)
        pool.affine_select(out=grp, in_=grp, compare_op=ALU.is_ge, fill=0.0, base=GROUP - 1,
                           pattern=[[GROUP, P // GROUP], [0, GROUP]],
                           channel_multiplier=-1).then_inc(const_ok, 1)

        pool.wait_ge(half_ok, 1)

        def scale_and_bias(n):
            pool.wait_ge(var_ok, n + 1)
            v, r0, t = SM[:, n, 2:3], RS[:, 0:1], RS[:, 1:2]

            def step(k, into, a, b, op=ALU.mult):
                pool.tensor_tensor(into, a, b, op).then_inc(rstd_ok, 1)
                pool.wait_ge(rstd_ok, RSTD_STEPS * n + k)

            step(1, r0, v, HALF, ALU.pow)
            step(2, t, r0, r0)
            step(3, t, t, v)
            pool.tensor_scalar(t, t, -0.5 * XS, 1.5 * XS, ALU.mult, ALU.add).then_inc(rstd_ok, 1)
            pool.wait_ge(rstd_ok, RSTD_STEPS * n + 4)
            step(5, SC[:, n, 0:1], r0, t)
            pool.tensor_tensor(SC[:, n, 1:2], SM[:, n, 3:4], SC[:, n, 0:1], ALU.mult
                               ).then_inc(norm_ok, 1)

        def low_parts(g):
            q = NCH * g
            with pool.Fori(0, NCH // 2) as i:
                for k in range(2):
                    pool.wait_ge(xn_ok, i * 2 + (q + k + 1))
                    pool.wait_ge(hi_ok, i * 2 + (q + k + 1))
                    rows = ds(i * 2 * TC + k * TC, TC)
                    pool.tensor_tensor(
                        XN[g % 2][:, 1, rows, 1:NW + 1],
                        SCR[:, k].rearrange("p (t w) -> p t w", w=NW),
                        XN[g % 2][:, 0, rows, 1:NW + 1], ALU.subtract).then_inc(lo_ok, 1)

        scale_and_bias(0)
        low_parts(0)
        scale_and_bias(1)
        for g in range(8):
            if g < 7:
                low_parts(g + 1)
            for n in FINISH[g]:
                scale_and_bias(n)
            if g < 2:
                pool.wait_ge(cw_in[g + 1], 16 * CW_DMAS)
                pool.wait_ge(msk_ok, KY)
                pool.wait_ge(cwt_zero, 1)
                build_matrices(pool, g + 1)
        scale_and_bias(11)
        scale_and_bias(12)
        for g in range(8, 12):
            low_parts(g)
            for n in FINISH[g]:
                scale_and_bias(n)

    @block.scalar
    def _(act):
        for l in range(3):
            for c in range(NC):
                act.dma_start(TW[c * R:(c + 1) * R, l].rearrange("p x y o -> p (x y o)"),
                              cw[l][c].rearrange("x y o -> (x y o)").unsqueeze(0)
                              .broadcast_to([R, KX * KY * NC])
                              ).then_inc(cw_in[l], 16)
            if l == 0:
                act.wait_ge(hw_zero, 1)
            for h in range(2):
                for side in range(2):
                    row = h * HROWS + side * NC * KX
                    act.dma_start(HW_[row:row + NC * KX, l, :, (R - 1) * side],
                                  cw[l][:, :, 2 * side].rearrange("c k o -> (c k) o"),
                                  allow_slow_non_contiguous=True
                                  ).then_inc(cw_in[l], 16)
            act.dma_start(BR[ONES:KH, l], cb[l].unsqueeze(0)).then_inc(cw_in[l], 16)
        act.dma_start(BB[0:FT * NE], b1.rearrange("e (t p) -> (e t) p", p=P)
                      ).then_inc(bb_in, 16)
        act.dma_start(BB[FT * NE:(FT + DH) * NE], b2.rearrange("e (t p) -> (e t) p", p=P)
                      ).then_inc(bb_in, 16)

        def normalise(g):
            n, b, q = stat_of_step(g), image_of_step(g), NCH * g
            act.wait_ge(norm_ok, n + 1)
            if g >= 2:
                act.wait_ge(conv_mm, NCH * (g - 1))
            if g == 8:
                act.wait_ge(hid_ok, NE * NPAIR * FT)
            if g in (8, 9):
                act.wait_ge(g2_mm, 4 * (NE - 1) + 2 * (g - 7))

            def chunk(i, k):
                src = X[:, ds(i * 2 * CH + (b * IMG + k * CH), CH)]
                src3 = src.rearrange("p (t w) -> p t w", w=NW)
                act.activation(SCR[:, k], src, ACT.Identity, bias=SC[:, n, 1:2],
                               scale=SC[:, n, 0:1]).then_inc(xn_ok, 1)
                act.activation(XN[g % 2][:, 0, ds(i * 2 * TC + k * TC, TC), 1:NW + 1], src3,
                               ACT.Identity, bias=SC[:, n, 1:2], scale=SC[:, n, 0:1]
                               ).then_inc(hi_ok, 1)

            if g == 0:
                for k in range(2):
                    chunk(0, k)
            with act.Fori(1 if g == 0 else 0, NCH // 2) as i:
                for k in range(2):
                    act.wait_ge(lo_ok, i * 2 + (q + k - 1))
                    chunk(i, k)

        def pre_chunk(b, j):
            m = NCH * b + j
            if j == 0:
                act.wait_ge(norm_ok, 8 + b + 1)
            if m >= 4:
                act.wait_ge(pre_mm, m - 3)
            act.activation(PRE[:, m % 4], X[:, b * IMG + j * CH:b * IMG + (j + 1) * CH],
                           ACT.Identity, bias=SC[:, 8 + b, 1:2], scale=SC[:, 8 + b, 0:1]
                           ).then_inc(pre_ok, 1)

        def xt_high(b, j):
            m = NCH * b + j
            act.wait_ge(pre_mm, m + 1)
            act.copy(xt_part(b, j, 0), tr_bank(m)).then_inc(xt_hi, 1)

        def prepare(b):
            for j in range(NCH + 1):
                if j < NCH:
                    pre_chunk(b, j)
                if j >= 1:
                    xt_high(b, j - 1)

        def split_high(src, dst, landed, made, e):
            act.wait_ge(landed, 16 * e + 16)
            act.activation(dst[:, 0], src[:], ACT.Copy, scale=WS).then_inc(made, 1)

        def gelu(e, ft, a):
            act.wait_ge(g1_mm, a + 1)
            act.activation(SCR[:, ft % 2], bank(ft % RING), ACT.Gelu,
                           bias=BT[:, ds(e * FT + ft, 1)], scale=1.0 / (XS * WS)
                           ).then_inc(gelu_ok, 1)

        def first_hidden():
            for ft in range(FT):
                if ft == 0:
                    act.wait_ge(lo_ok, NCH * 8)
                elif ft >= 2:
                    act.wait_ge(hid_ok, ft - 1)
                gelu(0, ft, ft)
                if ft >= 4:
                    for j in range(2 * ft - 8, 2 * ft - 6):
                        pre_chunk(3, j)
                    for j in range(2 * ft - 10, 2 * ft - 8 if ft < FT - 1 else NCH):
                        if j >= 0:
                            xt_high(3, j)
            act.wait_ge(pre_mm, NB * NCH)
            split_high(W2F, W2S, w2_in, w2_hi, 0)

        def hidden(e, p):
            for ft in range(FT):
                act.wait_ge(hid_ok, e * 16 + p * FT + (ft - 1))
                gelu(e, ft, e * 16 + p * FT + ft)

        def next_w1(e):
            act.wait_ge(g1_mm, e * 16)
            split_high(W1F, W1S, w1_in, w1_hi, e)

        def results(e):
            for p in range(NPAIR):
                for dh in range(DH):
                    act.wait_ge(g2_mm, e * 4 + (p * DH + dh + 1))
                    act.activation(
                        yt_part(e, p, dh),
                        bank(G2_BANK + dh).rearrange("p (t r) -> p t r", r=R),
                        ACT.Identity, bias=BT[:, ds(e * DH + (NE * FT + dh), 1)],
                        scale=1.0 / (HS * WS)).then_inc(yt_ok, 1)

        normalise(0)
        act.wait_ge(bt_mm, 1)
        act.copy(BT[:], bank(TR_BANK)[:, 0:(FT + DH) * NE]).then_inc(bt_ok, 1)
        for g in range(8):
            if g < 7:
                normalise(g + 1)
            if g == 7:
                split_high(W1F, W1S, w1_in, w1_hi, 0)
            if g >= 5:
                prepare(g - 5)
        act.wait_ge(bt_ok, 1)
        first_hidden()
        hidden(0, 1)
        next_w1(1)
        results(0)

        def expert(e):
            act.wait_ge(g2_mm, e * 4)
            split_high(W2F, W2S, w2_in, w2_hi, e)
            with act.Fori(0, NPAIR) as p:
                hidden(e, p)

        with act.Fori(1, NE - 1) as e:
            expert(e)
            next_w1(e + 1)
            results(e)
        expert(NE - 1)
        results(NE - 1)
        for g in range(8, 12):
            normalise(g)

    @block.vector
    def _(dve):
        bn_count = [0]

        def stats_chunk(n, src, slot):
            dve.bn_stats(ST[:, n % 2, slot], src).then_inc(bn_ok, 1)

        def aggregate(n):
            dve.wait_ge(bn_ok, bn_count[0])
            dve.bn_aggr(MV[:, n], ST[:, n % 2].rearrange("p c s -> p (c s)")
                        ).then_inc(mv_ok, 1)

        def deviation(n):
            dve.wait_ge(mean_mm, n + 1)
            mean = stat_psum(n, 0)
            dve.tensor_tensor(SM[:, n, 0:1], MV[:, n, 0:1], mean, ALU.subtract
                              ).then_inc(dev_ok, 1)
            dve.tensor_scalar(SM[:, n, 3:4], mean, -1.0, None, ALU.mult).then_inc(dev_ok, 1)
            dve.wait_ge(dev_ok, 2 * n + 2)
            dve.scalar_tensor_tensor(out=SM[:, n, 1:2], in0=SM[:, n, 0:1],
                                     scalar=SM[:, n, 0:1], in1=MV[:, n, 1:2],
                                     op0=ALU.mult, op1=ALU.add).then_inc(spread_ok, 1)

        def variance(n):
            dve.wait_ge(var_mm, n + 1)
            dve.tensor_scalar(SM[:, n, 2:3], stat_psum(n, 1), EPS, None, ALU.add
                              ).then_inc(var_ok, 1)

        def input_stats(b):
            for i in range(NCH):
                if b == 0 and i % (NCH // 2) == 0:
                    dve.wait_ge(x_in[i // (NCH // 2)], 16 * NC)
                elif i == 0:
                    dve.wait_ge(x_in[b + 1], 16 * NC)
                if i == 0 and b >= 2:
                    dve.wait_ge(mv_ok, b - 1)
                stats_chunk(b, X[:, b * IMG + i * CH:b * IMG + (i + 1) * CH], i)
            bn_count[0] += NCH
            aggregate(b)

        def conv_chunk(g, i, k, count):
            xc = X[:, ds(i * CH + image_of_step(g) * IMG, CH)]
            dve.wait_ge(conv_mm, i + (NCH * g + 1))
            dve.scalar_tensor_tensor(out=xc, in0=bank(k), scalar=1.0 / (XS * WS), in1=xc,
                                     op0=ALU.mult, op1=ALU.add).then_inc(x_new, 1)
            if g < 8:
                dve.wait_ge(x_new, count)
                stats_chunk(4 + g, xc, one(i))

        def conv_chunks(g, i0, i1):
            with dve.Fori(i0, i1) as i:
                conv_chunk(g, i, i - i0 // RING * RING, i + x_new_at[("c", g, 0)])
            bn_count[0] += i1 - i0 if g < 8 else 0

        def xt_low(b, j):
            m = NCH * b + j
            dve.wait_ge(xt_hi, m + 1)
            dve.tensor_tensor(xt_part(b, j, 1), tr_bank(m), xt_part(b, j, 0), ALU.subtract
                              ).then_inc(xt_lo, 1)

        def mlp_chunk(b, i):
            m = NCH * b + i
            xc = X[:, b * IMG + i * CH:b * IMG + (i + 1) * CH]
            dve.wait_ge(ty_mm, m + 1)
            dve.tensor_tensor(xc, bank(TR_BANK + m % 2), xc, ALU.add).then_inc(x_new, 1)
            dve.wait_ge(x_new, x_new_at[("y", b, i)])
            if i == 0:
                dve.wait_ge(mv_ok, 12 + b - 1)
            stats_chunk(12 + b, xc, i)
            bn_count[0] += 1

        def split_low(src, dst, landed, high, made, e):
            dve.wait_ge(landed, 16 * e + 16)
            dve.wait_ge(high, e + 1)
            dve.scalar_tensor_tensor(out=dst[:, 1], in0=src[:], scalar=WS, in1=dst[:, 0],
                                     op0=ALU.mult, op1=ALU.subtract).then_inc(made, 1)

        def zero_pads(s):
            dve.memset(XN[s][:, :, :, 0:PITCH:PITCH - 1], 0.0).then_inc(pads_ok[s], 1)

        def zero_halo(s, count):
            dve.memset(HALO[s][:].bitcast(U32), 0).then_inc(halo_ok[s], 1)
            dve.wait_ge(halo_ok[s], count)
            dve.memset(HALO[s][ONES:KH], XS).then_inc(halo_ok[s], 1)

        dve.memset(HW_[:], 0.0).then_inc(hw_zero, 1)
        dve.memset(CWT[:, :, 7], 0.0).then_inc(cwt_zero, 1)
        dve.wait_ge(const_ok, 8)
        for ky in range(KY):
            dve.tensor_reduce(MSK[:, ky], SEL[:, ky].rearrange("p c r -> p r c"), AX_X, ALU.add
                              ).then_inc(msk_ok, 1)
        for s in range(2):
            zero_pads(s)
            zero_halo(s, 1)
        dve.wait_ge(msk_ok, KY)
        dve.wait_ge(cwt_zero, 1)
        dve.wait_ge(cw_in[0], 16 * CW_DMAS)
        build_matrices(dve, 0)
        input_stats(0)
        deviation(0)
        variance(0)
        input_stats(1)
        deviation(1)
        variance(1)
        input_stats(2)
        for g in range(8):
            dve.wait_ge(mv_ok, 4 + g - 1)
            conv_chunks(g, 0, 2)
            for n in FINISH[g]:
                deviation(n)
            conv_chunks(g, 2, 4)
            for n in FINISH[g]:
                variance(n)
            if g < 5:
                conv_chunks(g, 4, NCH)
            else:
                if g == 7:
                    split_low(W1F, W1S, w1_in, w1_hi, w1_ok, 0)
                for i in range(4, NCH):
                    conv_chunk(g, i, i - RING, x_new_at[("c", g, i)])
                    bn_count[0] += 1
                    xt_low(g - 5, 2 * i - 8)
                    xt_low(g - 5, 2 * i - 7)
            if g == 0:
                input_stats(3)
            aggregate(4 + g)

        def expert(e, first):
            if not first:
                split_low(W2F, W2S, w2_in, w2_hi, w2_ok, e)
            for p in range(NPAIR):
                if not first:
                    dve.wait_ge(g2_mm, e * 4 + (2 * p - 2))
                for ft in range(FT):
                    a = e * 16 + (p * FT + ft)
                    dve.wait_ge(gelu_ok, a + 1)
                    dve.tensor_scalar(HID[p][:, 0, ft], SCR[:, ft % 2], HS, None, ALU.mult
                                      ).then_inc(hid_hi, 1)
                    dve.wait_ge(hid_hi, a + 1)
                    dve.scalar_tensor_tensor(out=HID[p][:, 1, ft], in0=SCR[:, ft % 2],
                                             scalar=HS, in1=HID[p][:, 0, ft], op0=ALU.mult,
                                             op1=ALU.subtract).then_inc(hid_ok, 1)
                    if first and p == 0:
                        if ft == 1:
                            deviation(11)
                        if ft == 3:
                            variance(11)
                        for j in range(2 * ft - 10, 2 * ft - 8 if ft < FT - 1 else NCH):
                            if j >= 0:
                                xt_low(3, j)
                    if first and p == 0 and ft == FT - 1:
                        split_low(W2F, W2S, w2_in, w2_hi, w2_ok, e)

        def next_w1(e):
            split_low(W1F, W1S, w1_in, w1_hi, w1_ok, e)

        expert(0, True)
        next_w1(1)
        with dve.Fori(1, NE - 1) as e:
            expert(e, False)
            next_w1(e + 1)
        expert(NE - 1, False)

        dve.wait_ge(w1_ok, NE)
        zero_halo(0, 3)
        dve.wait_ge(w2_ok, NE)
        zero_halo(1, 3)
        dve.wait_ge(g2_mm, 4 * (NE - 1) + 2)
        zero_pads(0)
        for i in range(NCH):
            mlp_chunk(0, i)
        aggregate(12)
        for i in range(2):
            mlp_chunk(1, i)
        deviation(12)
        for i in range(2, 4):
            mlp_chunk(1, i)
        variance(12)
        for i in range(4, NCH):
            mlp_chunk(1, i)
        aggregate(13)
        dve.wait_ge(g2_mm, 4 * NE)
        zero_pads(1)
        for g in range(8, 12):
            for i in range(NCH):
                if g < 10:
                    mlp_chunk(g - 6, i)
                conv_chunk(g, i, i % RING, 0)
                if i == 0:
                    for n in FINISH[g]:
                        deviation(n)
                if i == 1:
                    for n in FINISH[g]:
                        variance(n)
            if g < 10:
                aggregate(g + 6)

    @block.tensor
    def _(pe):
        averaged = [0]
        finished = [0]

        def group_mean(n):
            pe.wait_ge(mv_ok, n + 1)
            if n >= 1:
                pe.wait_ge(dev_ok, 2 * n)
            if finished[0]:
                pe.wait_ge(var_ok, finished[0])
            if n in (12, 13):
                if n == 12:
                    pe.wait_ge(gelu_ok, NE * NPAIR * FT)
                else:
                    pe.wait_ge(yt_ok, 4 * NE)
            pe.matmul(stat_psum(n, 0), GRP[:], MV[:, n, 0:1], start=True, stop=True
                      ).then_inc(mean_mm, 1)
            averaged[0] += 1

        def group_variance(n):
            pe.wait_ge(spread_ok, n + 1)
            pe.wait_ge(dev_ok, 2 * averaged[0])
            if finished[0]:
                pe.wait_ge(var_ok, finished[0])
            pe.matmul(stat_psum(n, 1), GRP[:], SM[:, n, 1:2], start=True, stop=True
                      ).then_inc(var_mm, 1)
            finished[0] += 1

        def conv_chunk(g, i, k):
            s, l = g % 2, g // 4
            acc = bank(k)
            pe.wait_ge(hi_ok, i + (NCH * g + 1))
            pe.wait_ge(lo_ok, i + (NCH * g + 1))
            n = 0
            for kx in range(KX):
                for part, w in ((0, kx), (1, kx), (0, 3 + kx)):
                    rhs = XN[s][:, part, ds(i * TC, TC), kx:kx + NW]
                    pe.matmul(acc, CWT[:, l, w], rhs, start=(n == 0), stop=False)
                    n += 1
            pe.wait_ge(halo_in[s], 64 * (g // 2 + 1))
            for w in (6, 7):
                rhs = HALO[s][0:KH, ds(i * TC, TC), 0:NW]
                mm = pe.matmul(acc, CWT[0:KH, l, w], rhs, start=False, stop=(w == 7))
            mm.then_inc(conv_mm, 1)

        def before_step(g):
            if g % 4 == 0:
                pe.wait_ge(build_ok[g // 4], BUILD_STEPS)
            pe.wait_ge(pads_ok[g % 2], 1 if g < 8 else 2)
            pe.wait_ge(halo_ok[g % 2], 2 if g < 8 else 4)

        def conv_chunks(g, i0, i1):
            before = [x_new_at.get(("c", g + (i - RING) // NCH, (i - RING) % NCH))
                      for i in range(i0, i1)]
            with pe.Fori(i0, i1) as i:
                if before[0] is not None:
                    stride = before[1] - before[0]
                    pe.wait_ge(x_new, i * stride + (before[0] - stride * i0))
                conv_chunk(g, i, i - i0 // RING * RING)

        def pre_transposes(b, j):
            m = NCH * b + j
            pe.wait_ge(pre_ok, m + 1)
            if m == 0:
                pe.wait_ge(bt_ok, 1)
            if m >= 2:
                pe.wait_ge(xt_lo, m - 1)
            to = bank(TR_BANK + m % 2)
            for h in range(DH):
                for t in range(TC):
                    mm = pe.transpose(to[:, (h * TC + t) * P:(h * TC + t + 1) * P],
                                      PRE[:, m % 4, t * NW + h * P:t * NW + (h + 1) * P], IDF[:])
            mm.then_inc(pre_mm, 1)

        def result_transposes(b, i):
            m = NCH * b + i
            if m < 2:
                pe.wait_ge(xt_lo, NB * NCH)
                pe.wait_ge(yt_ok, 4 * (NE - 1) + 2)
            else:
                pe.wait_ge(x_new, x_new_at[("y", (m - 2) // NCH, (m - 2) % NCH)])
            if b >= 2:
                pe.wait_ge(yt_ok, 4 * NE)
            to = bank(TR_BANK + m % 2)
            for t in range(TC):
                for h in range(DH):
                    tt = (b % 2) * NT + i * TC + t
                    mm = pe.transpose(to[:, t * NW + h * P:t * NW + (h + 1) * P],
                                      YT[:, b // 2, h, tt], IDF[:])
            mm.then_inc(ty_mm, 1)

        def hidden(e, p, first):
            for ft in range(FT):
                a = e * 16 + (p * FT + ft)
                if first and p == 0 and ft < RING:
                    pe.wait_ge(x_new, last_x_new(("c", 7)))
                else:
                    pe.wait_ge(gelu_ok, a - (RING - 1))
                if ft == 0:
                    pe.wait_ge(w1_ok, e + 1)
                    if first:
                        pe.wait_ge(xt_lo, 2 * NCH * (p + 1))
                n = 0
                for h in range(DH):
                    for part, w in ((0, 0), (1, 0), (0, 1)):
                        mm = pe.matmul(
                            bank(ft % RING),
                            W1S[:, w, h * NF + ft * P:h * NF + (ft + 1) * P],
                            XT[:, p, h, :, one(e), part], start=(n == 0),
                            stop=(n == 3 * DH - 1))
                        n += 1
                mm.then_inc(g1_mm, 1)
                if first and p == 0:
                    if ft == 1:
                        group_mean(11)
                    if ft == 3:
                        group_variance(11)
                    if ft >= 5:
                        for j in range(2 * ft - 10, 2 * ft - 8 if ft < FT - 1 else NCH):
                            pre_transposes(3, j)

        def output(e, p, h, between=None):
            k = p * DH + h
            if isinstance(e, int) and 4 * e + k < 2:
                pe.wait_ge(var_ok, 12)
            else:
                pe.wait_ge(yt_ok, e * 4 + (k - 1))
            for ft in range(FT):
                if h == 0:
                    pe.wait_ge(hid_ok, e * 16 + (p * FT + ft + 1))
                if ft == 0 and k == 0:
                    pe.wait_ge(w2_ok, e + 1)
                for part, w in ((0, 0), (1, 0), (0, 1)):
                    mm = pe.matmul(bank(G2_BANK + h),
                                   W2S[:, w, ft * NW + h * P:ft * NW + (h + 1) * P],
                                   HID[p][:, part, ft],
                                   start=(ft == 0 and part == 0 and w == 0),
                                   stop=(ft == FT - 1 and w == 1))
                if between is not None:
                    if ft == FT - 1:
                        mm.then_inc(g2_mm, 1)
                    between(ft)
            if between is None:
                mm.then_inc(g2_mm, 1)

        def expert(e, first):
            for p in range(NPAIR):
                hidden(e, p, first)
            for p in range(NPAIR):
                for h in range(DH):
                    output(e, p, h)

        pe.wait_ge(const_ok, 10)
        pe.wait_ge(bb_in, 32)
        nb = (FT + DH) * NE
        pe.transpose(bank(TR_BANK)[:, 0:nb], BB[:], IDF[0:nb, 0:nb]).then_inc(bt_mm, 1)
        pe.wait_ge(const_ok, 11)
        for n in range(2):
            group_mean(n)
            group_variance(n)
        for g in range(8):
            before_step(g)
            conv_chunks(g, 0, 2)
            for n in FINISH[g]:
                group_mean(n)
            conv_chunks(g, 2, 4)
            for n in FINISH[g]:
                group_variance(n)
            if g < 5:
                conv_chunks(g, 4, NCH)
            else:
                for i in range(4, NCH):
                    pe.wait_ge(x_new, x_new_at[("c", g, i - RING)])
                    conv_chunk(g, i, i - RING)
                    pre_transposes(g - 5, 2 * i - 8)
                    pre_transposes(g - 5, 2 * i - 7)
        expert(0, True)
        with pe.Fori(1, NE - 1) as e:
            expert(e, False)
        e = NE - 1
        hidden(e, 0, False)
        hidden(e, 1, False)
        output(e, 0, 0)
        output(e, 0, 1)
        output(e, 1, 0, lambda ft: result_transposes(0, ft))

        result_transposes(1, 0)
        result_transposes(1, 1)
        group_mean(12)
        result_transposes(1, 2)
        result_transposes(1, 3)
        group_variance(12)
        output(e, 1, 1, lambda ft: result_transposes(1, ft + 4) if ft < 4 else None)
        for g in range(8, 12):
            before_step(g)
            for i in range(NCH):
                if g < 10:
                    result_transposes(g - 6, i)
                if g == 8 and i == 0:
                    pe.wait_ge(var_ok, 13)
                if g > 8 or i >= RING:
                    pe.wait_ge(x_new, x_new_at[("c", g + (i - RING) // NCH, (i - RING) % NCH)])
                else:
                    pe.wait_ge(gelu_ok, NE * NPAIR * FT)
                conv_chunk(g, i, i % RING)
                for n in FINISH[g]:
                    if i == 0:
                        group_mean(n)
                    if i == 1:
                        group_variance(n)

    ctx.close()


INPUTS = ["x", "L0_conv_weight", "L0_conv_bias", "L1_conv_weight", "L1_conv_bias", "L2_conv_w1",
          "L2_conv_b1", "L2_conv_w2", "L2_conv_b2", "L3_conv_weight", "L3_conv_bias"]


def kernel(**inputs):
    import concourse.bacc as bacc
    import numpy as np
    from concourse.bass_utils import run_bass_kernel_spmd

    nc = bacc.Bacc("TRN2", target_bir_lowering=False, num_devices=1)
    arrays, t = {}, {}
    for name in INPUTS:
        a = np.asarray(inputs[name])
        if name.endswith("conv_weight"):
            a = a.transpose(1, 3, 2, 0)
        arrays[name] = np.ascontiguousarray(a)
        t[name] = nc.dram_tensor(name, arrays[name].shape, F32, kind="ExternalInput").ap()
    out = nc.dram_tensor("out", (NB, NC, NH, NW), F32, kind="ExternalOutput").ap()
    convs = ("L0", "L1", "L3")
    bass_program(nc, t["x"], [t[f"{l}_conv_weight"] for l in convs],
                 [t[f"{l}_conv_bias"] for l in convs], t["L2_conv_w1"], t["L2_conv_b1"],
                 t["L2_conv_w2"], t["L2_conv_b2"], out)
    return run_bass_kernel_spmd(nc, [arrays], core_ids=[0]).results[0]["out"]
```

```python
from contextlib import ExitStack

import concourse.bass as bass
from concourse import mybir

ALU = mybir.AluOpType
ACT = mybir.ActivationFunctionType
F32 = mybir.dt.float32
F16 = mybir.dt.float16
U32 = mybir.dt.uint32
AX_X = mybir.AxisListType.X
ds = bass.ds

P = 128
NB, NC, NH, NW = 4, 8, 256, 256
R = P // NC
NT = NH // R
IMG = NT * NW
CH = 512
NCH = IMG // CH
TC = CH // NW
PITCH = NW + 2
GROUP = 2 * R
EPS = 1e-5
NE, NF = 8, 1024
FT = NF // P
DH = NW // P
NPAIR = NB // 2
TT = 2 * NT
KX = KY = 3
HROWS = 2 * NC * KX
ONES = 2 * HROWS
KH = ONES + 1
XS, WS, HS = 64.0, 256.0, 16.0

FINISH = {0: [1], 1: [2, 3], 2: [4, 5], 3: [6], 4: [7], 5: [8], 6: [9], 7: [10],
          8: [13, 14], 9: [15], 10: [], 11: []}
RESULTS_AT = [[0], [1], [2], [3], [4], [5], [6, 7], []]
PREP_AT = {5: 4, 6: 4, 7: 3}
SLOTS = {1: (2, 3), 2: (0, 3), 3: (4, 6), 4: (2, 3), 5: (4, 5), 6: (3, 5), 7: (3, 5),
         8: (0, 1), 9: (0, 1), 10: (0, 1), 13: (0, 1), 14: (6, 7), 15: (6, 7)}


def finishing(g, i, second):
    return [n for n in FINISH[g] if SLOTS[n][second] == i]


def stat_of_step(g):
    return g if g < 8 else g + 4


def image_of_step(g):
    return g % 4


RSTD_STEPS = 5
WROWS = NC * KX + 1


def bass_program(nc, x, cw, cb, w1, b1, w2, b2, out):
    ctx = ExitStack()

    def at(name, offset, shape, dt):
        return nc.alloc_sbuf_tensor_at(name, shape, dt, offset=offset)

    def sem(name):
        return nc.alloc_semaphore(name)

    base = (nc.sbuf_base + 31) // 32 * 32
    X_OFF = base
    XY_OFF = X_OFF + NB * IMG * 4
    XN_OFF = XY_OFF + NB * IMG * 4
    XN_SLOT = 2 * NT * PITCH * 2
    HALO_OFF = XN_OFF + 2 * XN_SLOT
    HALO_SLOT = NT * PITCH * 2
    W1S_OFF = HALO_OFF + 2 * HALO_SLOT
    W2S_OFF = W1S_OFF + 2 * DH * NF * 2
    CW_OFF = W2S_OFF + 2 * FT * NW * 2
    SCR_OFF = CW_OFF + 3 * 2 * 4 * P * 2
    C_OFF = SCR_OFF + 2 * CH * 4

    X = at("X", X_OFF, [P, NB * IMG], F32)
    XT = at("XT", XY_OFF, [P, NPAIR, DH, TT, NC, 2, R], F16)
    YT = at("YT", XY_OFF, [P, NPAIR, DH, TT, NC * R], F32)
    XN = [at(f"XN{s}", XN_OFF + s * XN_SLOT, [P, 2, NT, PITCH], F16) for s in range(2)]
    HALO = [at(f"HALO{s}", HALO_OFF + s * HALO_SLOT, [P, NT, PITCH], F16) for s in range(2)]
    HID = [at(f"HID{p}", XN_OFF + p * XN_SLOT, [P, 2, FT, CH], F16) for p in range(NPAIR)]
    W1F = at("W1F", HALO_OFF, [P, DH * NF], F32)
    W2F = at("W2F", HALO_OFF + HALO_SLOT, [P, FT * NW], F32)
    W1S = at("W1S", W1S_OFF, [P, 2, DH * NF], F16)
    W2S = at("W2S", W2S_OFF, [P, 2, FT * NW], F16)
    PRE = at("PRE", W2S_OFF, [P, 4, CH], F32)
    PRE3 = at("PRE3", XN_OFF + XN_SLOT, [P, NCH, CH], F32)
    CWT = at("CWT", CW_OFF, [P, 3, 2, 4, P], F16)
    SCR = at("SCR", SCR_OFF, [P, 2, CH], F32)
    o = C_OFF
    IDF = at("IDF", o, [P, P], F32); o += P * 4
    GRP = at("GRP", o, [P, P], F32); o += P * 4
    BT = at("BT", o, [P, (FT + DH) * NE], F32); o += (FT + DH) * NE * 4
    ST = at("ST", o, [P, 4, NCH, 6], F32); o += 4 * NCH * 6 * 4
    MV = at("MV", o, [P, 16, 2], F32); o += 16 * 2 * 4
    SM = at("SM", o, [P, 16, 4], F32); o += 16 * 4 * 4
    SC = at("SC", o, [P, 16, 2], F32); o += 16 * 2 * 4
    RS = at("RS", o, [P, 8], F32); o += 32
    HALF = RS[:, 2:3]
    assert o <= nc.sbuf_usable_end, (o, nc.sbuf_usable_end)
    s0 = XY_OFF
    WK = at("WK", s0, [WROWS, 3, KY, NC], F32); s0 += 3 * KY * NC * 4
    SELW = at("SELW", s0, [WROWS, 4, P], F32); s0 += 4 * P * 4
    BLK = at("BLK", s0, [P, NC, R], F32); s0 += P * 4
    BAND = at("BAND", s0, [P, KY, NC, R], F32); s0 += NC * KY * R * 4
    EDGE = at("EDGE", s0, [P, 2, 2, R], F32); s0 += 4 * R * 4
    MSK = at("MSK", s0, [P, 4, KY, R], F32); s0 += 4 * KY * R * 4
    ACC = at("ACC", s0, [P, 4, NC, R], F32); s0 += 4 * P * 4
    TMP = at("TMP", s0, [P, 4, NC, R], F32); s0 += 4 * P * 4
    BB = at("BB", s0, [(FT + DH) * NE, P], F32)

    PS = nc.alloc_psum_tensor("PS", [P, 8 * CH], F32)
    RING, G2_BANK, TR_BANK = 4, 4, 6

    def bank(k):
        return PS[:, ds(k * CH, CH)] if not isinstance(k, int) else PS[:, k * CH:(k + 1) * CH]

    def stat_psum(n, col):
        k = 0 if n == 12 else G2_BANK + n % 2
        return PS[:, k * CH + col:k * CH + col + 1]

    TAPS = PS[:, TR_BANK * CH:TR_BANK * CH + 4 * 3 * KY * NC].rearrange(
        "p (s l y o) -> p s l y o", s=4, l=3, y=KY)

    def tr_bank(m):
        return bank(TR_BANK + m % 2).rearrange("p (h t c r) -> p h (t c) r", h=DH, t=TC, c=NC)

    def pre(b, j):
        return PRE[:, j % 4] if b < NB - 1 else PRE3[:, j]

    def xt_part(b, j, h):
        tt = (b % 2) * NT + j * TC
        return XT[:, b // 2, :, tt:tt + TC, :, h, :].rearrange("p h t c r -> p h (t c) r")

    def yt_part(e, p, dh):
        return YT[:, p, dh, :, ds(e * R, R)]

    x0_in = [sem(f"x0_in{i}") for i in range(NCH)]
    x_in = [sem(f"x_in{b}") for b in range(NB)]
    cw_in = sem("cw_in")
    bb_in = sem("bb_in")
    halo_first = sem("halo_first")
    halo_in = [sem(f"halo_in{s}") for s in range(2)]
    w1_in, w2_in = sem("w1_in"), sem("w2_in")
    out_done = sem("out_done")
    const_ok = sem("const_ok")
    wk_zero = sem("wk_zero")
    msk_ok = sem("msk_ok")
    taps_mm = sem("taps_mm")
    pads_ok = [sem(f"pads_ok{s}") for s in range(2)]
    halo_ok = [sem(f"halo_ok{s}") for s in range(2)]
    build_ok = [sem(f"build_ok{l}") for l in range(3)]
    bt_mm, bt_ok = sem("bt_mm"), sem("bt_ok")
    bn_ok = sem("bn_ok")
    mv_in = sem("mv_in")
    mv_ok = sem("mv_ok")
    mean_mm = sem("mean_mm")
    dev_ok = sem("dev_ok")
    spread_ok = sem("spread_ok")
    var_mm = sem("var_mm")
    var_ok = sem("var_ok")
    rstd_ok = sem("rstd_ok")
    half_ok = sem("half_ok")
    norm_ok = sem("norm_ok")
    xn_ok = sem("xn_ok")
    hi_ok = sem("hi_ok")
    lo_ok = sem("lo_ok")
    conv_mm = sem("conv_mm")
    x_new = sem("x_new")
    pre_ok = sem("pre_ok")
    pre_mm = sem("pre_mm")
    xt_hi = sem("xt_hi")
    xt_lo = sem("xt_lo")
    w1_hi, w1_ok = sem("w1_hi"), sem("w1_ok")
    w2_hi, w2_ok = sem("w2_hi"), sem("w2_ok")
    g1_mm = sem("g1_mm")
    gelu_ok = sem("gelu_ok")
    hid_hi, hid_ok = sem("hid_hi"), sem("hid_ok")
    g2_mm = sem("g2_mm")
    yt_ok = sem("yt_ok")
    ty_mm = sem("ty_mm")

    block = ctx.enter_context(nc.Block())

    order = [("c", g, i) for g in range(8) for i in range(NCH)]
    order += [("y", b, i) for b in range(2) for i in range(NCH)]
    order += [("y", 2, i) for i in range(NCH)] + [("c", 8, i) for i in range(NCH)]
    for i in range(NCH):
        order += [("y", 3, 2 * i + k) for k in range(2) if i < NCH // 2] + [("c", 9, i)]
    order += [("c", g, i) for g in (10, 11) for i in range(NCH)]
    x_new_at = {k: n + 1 for n, k in enumerate(order)}

    def aggregated(n):
        return (mv_in, n + 1) if n < NB else (mv_ok, n - NB + 1)

    def last_x_new(key):
        return x_new_at[(key[0], key[1], NCH - 1)]

    @block.sync
    def _(sp):
        def move_image(b, t0, t1, store, signal):
            for c in range(NC):
                sb = X[c * R:(c + 1) * R, b * IMG + t0 * NW:b * IMG + t1 * NW]
                sb = sb.rearrange("r (t w) -> r t w", w=NW)
                dr = (out if store else x)[b, c].rearrange("(t r) w -> r t w", r=R)[:, t0:t1]
                sp.dma_start(dr if store else sb, sb if store else dr).then_inc(signal, 16)

        def move_tile(b, t, store, signal):
            sb = X[:, b * IMG + t * NW:b * IMG + (t + 1) * NW]
            dr = (out if store else x)[b, :, t * R:(t + 1) * R]
            sp.dma_start(dr if store else sb, sb if store else dr).then_inc(signal, 16)

        for t in range(NT):
            move_tile(0, t, False, x0_in[t // TC])
        for b in range(1, NB):
            move_image(b, 0, NT, False, x_in[b])

        def shifted_rows(s, h, side, t0, nt, signal):
            run = (nt - 1) * PITCH + NW
            src = XN[s][(R - 1) * (1 - side):P:R, h, t0 - 1 + 2 * side:]
            src = src.rearrange("p t w -> p (t w)")
            src = bass.AP(src.tensor, src.offset, [src.ap[0], (1, KX), (1, run)])
            dst = HALO[s][:].rearrange("p t w -> p (t w)")
            row = h * HROWS + side * NC * KX
            sp.dma_start(dst[row:row + NC * KX, t0 * PITCH:t0 * PITCH + run], src
                         ).then_inc(signal, 16)

        def halos(g):
            s = g % 2
            if g >= 2:
                sp.wait_ge(conv_mm, NCH * (g - 1))
            sp.wait_ge(pads_ok[s], 1 if g < 8 else 2)
            sp.wait_ge(halo_ok[s], 2 if g < 8 else 4)
            half = NT // 2
            if g == 0:
                for h in range(2):
                    sp.wait_ge(hi_ok if h == 0 else lo_ok, NCH // 2 + 1)
                    shifted_rows(s, h, 0, 1, half - 1, halo_first)
                    shifted_rows(s, h, 1, 0, half, halo_first)
            for h in range(2):
                sp.wait_ge(hi_ok if h == 0 else lo_ok, NCH * (g + 1))
                for side in range(2):
                    t0 = half if g == 0 else 1 - side
                    t1 = NT - side
                    shifted_rows(s, h, side, t0, t1 - t0, halo_in[s])

        def load_w1(e):
            if e > 0:
                sp.wait_ge(w1_ok, e)
            sp.dma_start(W1F[:].rearrange("p (h f) -> p h f", h=DH),
                         w1[e].rearrange("(h p) f -> p h f", p=P)).then_inc(w1_in, 16)

        def load_w2(e):
            if e > 0:
                sp.wait_ge(w2_ok, e)
            sp.dma_start(W2F[:].rearrange("p (h d) -> p h d", h=FT),
                         w2[e].rearrange("(h p) d -> p h d", p=P)).then_inc(w2_in, 16)

        for g in range(8):
            halos(g)
        sp.wait_ge(conv_mm, NCH * 7)
        load_w1(0)
        sp.wait_ge(conv_mm, NCH * 8)
        load_w2(0)
        for e in range(1, NE):
            load_w1(e)
            load_w2(e)
        for g in range(8, 12):
            halos(g)
            if g >= 9:
                sp.wait_ge(x_new, last_x_new(("c", g - 1)))
                move_image(g - 9, 0, NT, True, out_done)
        for i in range(NCH):
            sp.wait_ge(x_new, x_new_at[("c", 11, i)])
            for t in range(TC * i, TC * (i + 1)):
                move_tile(NB - 1, t, True, out_done)
        sp.wait_ge(out_done, 16 * (NC * (NB - 1) + NT))

    SELW_MADE, MASKS_MADE, CONSTS_MADE = 8, 16, 19
    ONES_BITS = 0x54005400
    BUILD_STEPS = 2 * KY + 1

    @block.gpsimd
    def _(pool):
        def set_ones(s):
            pool.memset(HALO[s][ONES:KH].bitcast(U32), ONES_BITS).then_inc(halo_ok[s], 1)

        pool.memset(HALF, -0.5).then_inc(half_ok, 1)
        pool.memset(WK[:], 0.0).then_inc(wk_zero, 1)
        pool.memset(SELW[:], 0.0).then_inc(const_ok, 1)
        pool.memset(BLK[:], 1.0).then_inc(const_ok, 1)
        pool.memset(EDGE[:], 1.0).then_inc(const_ok, 1)
        pool.memset(GRP[:], 1.0 / GROUP).then_inc(const_ok, 1)
        pool.memset(IDF[:], 0.0).then_inc(const_ok, 1)
        made = [5]

        def select(into, pattern, base, mult, op, fill, src=None):
            pool.wait_ge(const_ok, made[0])
            pool.affine_select(out=into, in_=into if src is None else src, compare_op=op,
                               fill=fill, base=base, pattern=pattern, channel_multiplier=mult
                               ).then_inc(const_ok, 1)
            made[0] += 1

        select(SELW[:, 0:KX].rearrange("k x (c r) -> k x c r", r=R),
               [[-1, KX], [-KX, NC], [0, R]], 0, 1, ALU.not_equal, 1.0)
        select(SELW[:, 3, 0:ONES].rearrange("k (h j) -> k h j", j=NC * KX),
               [[0, 4], [-1, NC * KX]], 0, 1, ALU.not_equal, 1.0)
        select(SELW[:, 3, ONES:KH], [[0, 1]], -NC * KX, 1, ALU.not_equal, 1.0)
        select(BLK[:], [[-R, NC], [0, R]], 0, 1, ALU.is_ge, 0.0)
        select(BLK[:], [[R, NC], [0, R]], R - 1, -1, ALU.is_ge, 0.0)
        for ky in range(KY):
            select(BAND[:, ky], [[-R, NC], [-1, R]], 1 - ky, 1, ALU.is_equal, 0.0, BLK[:])
        select(EDGE[:], [[-HROWS, 2], [-NC * KX, 2], [0, R]], 0, 1, ALU.is_ge, 0.0)
        select(EDGE[:], [[HROWS, 2], [NC * KX, 2], [0, R]], NC * KX - 1, -1, ALU.is_ge, 0.0)
        select(EDGE[:], [[0, 2], [-(R - 1), 2], [1, R]], 0, 0, ALU.is_equal, 0.0)
        masks_made = made[0]
        grp = GRP[:].rearrange("p (g k) -> p g k", k=GROUP)
        select(grp, [[-GROUP, P // GROUP], [0, GROUP]], 0, 1, ALU.is_ge, 0.0)
        select(grp, [[GROUP, P // GROUP], [0, GROUP]], GROUP - 1, -1, ALU.is_ge, 0.0)
        select(IDF[:], [[-1, P]], 0, 1, ALU.not_equal, 1.0)
        assert (masks_made, made[0]) == (MASKS_MADE, CONSTS_MADE)
        pool.wait_ge(const_ok, CONSTS_MADE)
        set_ones(1)
        pool.wait_ge(halo_ok[1], 2)
        pool.wait_ge(half_ok, 1)

        def scale_and_bias(n):
            pool.wait_ge(var_ok, n + 1)
            v, r0, t = SM[:, n, 2:3], RS[:, 0:1], RS[:, 1:2]

            def step(k, into, a, b, op=ALU.mult):
                pool.tensor_tensor(into, a, b, op).then_inc(rstd_ok, 1)
                pool.wait_ge(rstd_ok, RSTD_STEPS * n + k)

            step(1, r0, v, HALF, ALU.pow)
            step(2, t, r0, r0)
            step(3, t, t, v)
            pool.tensor_scalar(t, t, -0.5 * XS, 1.5 * XS, ALU.mult, ALU.add).then_inc(rstd_ok, 1)
            pool.wait_ge(rstd_ok, RSTD_STEPS * n + 4)
            step(5, SC[:, n, 0:1], r0, t)
            pool.tensor_tensor(SC[:, n, 1:2], SM[:, n, 3:4], SC[:, n, 0:1], ALU.mult
                               ).then_inc(norm_ok, 1)

        def low_parts(g, i0=0, i1=NCH // 2):
            q = NCH * g
            with pool.Fori(i0, i1) as i:
                for k in range(2):
                    pool.wait_ge(xn_ok, i * 2 + (q + k + 1))
                    pool.wait_ge(hi_ok, i * 2 + (q + k + 1))
                    rows = ds(i * 2 * TC + k * TC, TC)
                    pool.tensor_tensor(
                        XN[g % 2][:, 1, rows, 1:NW + 1],
                        SCR[:, k].rearrange("p (t w) -> p t w", w=NW),
                        XN[g % 2][:, 0, rows, 1:NW + 1], ALU.subtract).then_inc(lo_ok, 1)

        scale_and_bias(0)
        low_parts(0)
        scale_and_bias(1)
        low_parts(1)
        scale_and_bias(2)
        low_parts(2)
        scale_and_bias(3)
        for g in range(2, 5):
            low_parts(g + 1)
            for n in FINISH[g]:
                scale_and_bias(n)
        for g in (5, 6):
            low_parts(g + 1, 0, NCH // 4)
            scale_and_bias(g + 3)
            low_parts(g + 1, NCH // 4)
        scale_and_bias(10)
        scale_and_bias(11)
        pool.wait_ge(norm_ok, 12)
        pool.wait_ge(w1_ok, NE)
        set_ones(0)
        pool.wait_ge(halo_ok[0], 4)
        pool.wait_ge(w2_ok, NE)
        set_ones(1)
        pool.wait_ge(halo_ok[1], 4)
        scale_and_bias(12)
        low_parts(8)
        scale_and_bias(13)
        low_parts(9)
        scale_and_bias(14)
        low_parts(10)
        scale_and_bias(15)
        low_parts(11)

    @block.scalar
    def _(act):
        act.wait_ge(wk_zero, 1)
        act.dma_start(WK[0:WROWS - 1], cw.rearrange("c x l y o -> (c x) l y o")
                      ).then_inc(cw_in, 16)
        act.dma_start(WK[WROWS - 1:WROWS, :, 0], cb.unsqueeze(0)).then_inc(cw_in, 16)
        act.wait_ge(x0_in[0], 16 * TC)
        act.dma_start(BB[0:FT * NE], b1.rearrange("e (t p) -> (e t) p", p=P)
                      ).then_inc(bb_in, 16)
        act.dma_start(BB[FT * NE:(FT + DH) * NE], b2.rearrange("e (t p) -> (e t) p", p=P)
                      ).then_inc(bb_in, 16)

        def normalise(g, i0=0, i1=NCH // 2):
            n, b, q = stat_of_step(g), image_of_step(g), NCH * g
            if i0 == 0:
                act.wait_ge(norm_ok, n + 1)
                if g >= 2:
                    act.wait_ge(conv_mm, NCH * (g - 1))
                if g == 8:
                    act.wait_ge(hid_ok, NE * NPAIR * FT)
                if g in (8, 9):
                    act.wait_ge(g2_mm, 4 * (NE - 1) + 2 * (g - 7))

            def chunk(i, k):
                src = X[:, ds(i * 2 * CH + (b * IMG + k * CH), CH)]
                src3 = src.rearrange("p (t w) -> p t w", w=NW)
                act.activation(SCR[:, k], src, ACT.Identity, bias=SC[:, n, 1:2],
                               scale=SC[:, n, 0:1]).then_inc(xn_ok, 1)
                act.activation(XN[g % 2][:, 0, ds(i * 2 * TC + k * TC, TC), 1:NW + 1], src3,
                               ACT.Identity, bias=SC[:, n, 1:2], scale=SC[:, n, 0:1]
                               ).then_inc(hi_ok, 1)

            if g == 0:
                for k in range(2):
                    chunk(0, k)
                i0 = 1
            with act.Fori(i0, i1) as i:
                for k in range(2):
                    act.wait_ge(lo_ok, i * 2 + (q + k - 1))
                    chunk(i, k)

        def pre_chunk(b, j):
            m = NCH * b + j
            if j == 0:
                act.wait_ge(norm_ok, 8 + b + 1)
            if b < NB - 1:
                if m >= 4:
                    act.wait_ge(pre_mm, m - 3)
            elif j == 0:
                act.wait_ge(conv_mm, NCH * 8)
            act.activation(pre(b, j), X[:, b * IMG + j * CH:b * IMG + (j + 1) * CH],
                           ACT.Identity, bias=SC[:, 8 + b, 1:2], scale=SC[:, 8 + b, 0:1]
                           ).then_inc(pre_ok, 1)

        def xt_high(b, j):
            m = NCH * b + j
            act.wait_ge(pre_mm, m + 1)
            act.copy(xt_part(b, j, 0), tr_bank(m)).then_inc(xt_hi, 1)

        def split_high(src, dst, landed, made, e):
            act.wait_ge(landed, 16 * e + 16)
            act.activation(dst[:, 0], src[:], ACT.Copy, scale=WS).then_inc(made, 1)

        def gelu(e, ft, a):
            act.wait_ge(g1_mm, a + 1)
            act.activation(SCR[:, ft % 2], bank(ft % RING), ACT.Gelu,
                           bias=BT[:, ds(e * FT + ft, 1)], scale=1.0 / (XS * WS)
                           ).then_inc(gelu_ok, 1)

        def first_hidden():
            for ft in range(FT):
                if ft == 0:
                    act.wait_ge(lo_ok, NCH * 8)
                elif ft >= 2:
                    act.wait_ge(hid_ok, ft - 1)
                gelu(0, ft, ft)
                if ft == 3:
                    act.wait_ge(pre_mm, (NB - 1) * NCH)
                    split_high(W2F, W2S, w2_in, w2_hi, 0)

        def last_hidden(e):
            for ft in range(FT):
                a = e * 16 + FT + ft
                act.wait_ge(hid_ok, a - 1)
                gelu(e, ft, a)
                act.wait_ge(gelu_ok, a + 1)
                act.activation(HID[1][:, 0, ft], SCR[:, ft % 2], ACT.Copy, scale=HS
                               ).then_inc(hid_hi, 1)

        def hidden(e, p):
            for ft in range(FT):
                act.wait_ge(hid_ok, e * 16 + p * FT + (ft - 1))
                gelu(e, ft, e * 16 + p * FT + ft)

        def next_w1(e):
            act.wait_ge(g1_mm, e * 16)
            split_high(W1F, W1S, w1_in, w1_hi, e)

        def result(e, p, dh):
            act.wait_ge(g2_mm, e * 4 + (p * DH + dh + 1))
            act.activation(
                yt_part(e, p, dh),
                bank(G2_BANK + dh).rearrange("p (t r) -> p t r", r=R),
                ACT.Identity, bias=BT[:, ds(e * DH + (NE * FT + dh), 1)],
                scale=1.0 / (HS * WS)).then_inc(yt_ok, 1)

        def results(e):
            for p in range(NPAIR):
                for dh in range(DH):
                    result(e, p, dh)

        normalise(0)
        act.wait_ge(bt_mm, 1)
        act.copy(BT[:], bank(TR_BANK + 1)[:, 0:(FT + DH) * NE]).then_inc(bt_ok, 1)
        for g in range(5):
            normalise(g + 1)
        for g in (5, 6):
            b = g - 5
            normalise(g + 1, 0, 2)
            for j in range(4):
                pre_chunk(b, j)
            for i in (2, 3):
                normalise(g + 1, i, i + 1)
                for j in (2 * i - 4, 2 * i - 3):
                    xt_high(b, j)
                    pre_chunk(b, j + 4)
            for j in range(4, NCH):
                xt_high(b, j)
        split_high(W1F, W1S, w1_in, w1_hi, 0)
        for j in range(NCH + 2):
            if j < NCH:
                pre_chunk(2, j)
            if j >= 2:
                xt_high(2, j - 2)
        act.wait_ge(bt_ok, 1)
        first_hidden()
        for j in range(2):
            pre_chunk(3, j)
        for j in range(NCH):
            if j < NCH - 2:
                pre_chunk(3, j + 2)
            xt_high(3, j)
            if j == NCH // 2:
                result(0, 0, 0)
        result(0, 0, 1)
        hidden(0, 1)
        next_w1(1)
        result(0, 1, 0)
        result(0, 1, 1)

        def expert(e):
            act.wait_ge(g2_mm, e * 4)
            split_high(W2F, W2S, w2_in, w2_hi, e)
            with act.Fori(0, NPAIR) as p:
                hidden(e, p)

        with act.Fori(1, NE - 1) as e:
            expert(e)
            next_w1(e + 1)
            results(e)
        e = NE - 1
        act.wait_ge(g2_mm, e * 4)
        split_high(W2F, W2S, w2_in, w2_hi, e)
        hidden(e, 0)
        result(e, 0, 0)
        result(e, 0, 1)
        last_hidden(e)
        normalise(8, 0, 3)
        result(e, 1, 0)
        result(e, 1, 1)
        normalise(8, 3, 4)
        for g in range(9, 12):
            normalise(g)

    @block.vector
    def _(dve):
        bn_count = [0]

        def stats_chunk(n, src, slot):
            dve.bn_stats(ST[:, n % 4, slot], src).then_inc(bn_ok, 1)

        def aggregate(n):
            dve.wait_ge(bn_ok, bn_count[0])
            dve.bn_aggr(MV[:, n], ST[:, n % 4].rearrange("p c s -> p (c s)")
                        ).then_inc(aggregated(n)[0], 1)

        def deviation(n):
            dve.wait_ge(mean_mm, n + 1)
            mean = stat_psum(n, 0)
            dve.tensor_tensor(SM[:, n, 0:1], MV[:, n, 0:1], mean, ALU.subtract
                              ).then_inc(dev_ok, 1)
            dve.tensor_scalar(SM[:, n, 3:4], mean, -1.0, None, ALU.mult).then_inc(dev_ok, 1)
            dve.wait_ge(dev_ok, 2 * n + 2)
            dve.scalar_tensor_tensor(out=SM[:, n, 1:2], in0=SM[:, n, 0:1],
                                     scalar=SM[:, n, 0:1], in1=MV[:, n, 1:2],
                                     op0=ALU.mult, op1=ALU.add).then_inc(spread_ok, 1)

        def variance(n):
            dve.wait_ge(var_mm, n + 1)
            dve.tensor_scalar(SM[:, n, 2:3], stat_psum(n, 1), EPS, None, ALU.add
                              ).then_inc(var_ok, 1)

        def input_stats(b, i0, i1):
            for i in range(i0, i1):
                if b == 0:
                    dve.wait_ge(x0_in[i], 16 * TC)
                else:
                    dve.wait_ge(x_in[b], 16 * NC)
                stats_chunk(b, X[:, b * IMG + i * CH:b * IMG + (i + 1) * CH], i)
            bn_count[0] += i1 - i0
            if i1 == NCH:
                aggregate(b)

        def build(l):
            done = [0]

            def step(ins):
                done[0] += 1
                ins.then_inc(build_ok[l], 1)
                dve.wait_ge(build_ok[l], done[0])

            dve.wait_ge(taps_mm, 4)
            dve.wait_ge(msk_ok, 4)
            for ky in range(KY):
                weight = TAPS[:, :, l, ky].unsqueeze(3).broadcast_to([P, 4, NC, R])
                mask = MSK[:, :, ky].unsqueeze(2).broadcast_to([P, 4, NC, R])
                step(dve.tensor_tensor(ACC[:] if ky == 0 else TMP[:], weight, mask, ALU.mult))
                if ky >= 1:
                    step(dve.tensor_tensor(ACC[:], ACC[:], TMP[:], ALU.add))
            acc = ACC[:].rearrange("p s c r -> p (s c r)")
            hi = CWT[:, l, 0].rearrange("p s m -> p (s m)")
            lo = CWT[:, l, 1].rearrange("p s m -> p (s m)")
            step(dve.tensor_scalar(hi, acc, WS, None, ALU.mult))
            step(dve.scalar_tensor_tensor(out=lo, in0=acc, scalar=WS, in1=hi, op0=ALU.mult,
                                          op1=ALU.subtract))

        def conv_chunk(g, i, k, count):
            xc = X[:, ds(i * CH + image_of_step(g) * IMG, CH)]
            dve.wait_ge(conv_mm, i + (NCH * g + 1))
            dve.scalar_tensor_tensor(out=xc, in0=bank(k), scalar=1.0 / (XS * WS), in1=xc,
                                     op0=ALU.mult, op1=ALU.add).then_inc(x_new, 1)
            if g < 8:
                dve.wait_ge(x_new, count)
                stats_chunk(4 + g, xc, i)

        def conv_chunks(g, i0, i1):
            with dve.Fori(i0, i1) as i:
                conv_chunk(g, i, i - i0 // RING * RING, i + x_new_at[("c", g, 0)])
            bn_count[0] += i1 - i0 if g < 8 else 0

        def xt_low(b, j):
            m = NCH * b + j
            dve.wait_ge(xt_hi, m + 1)
            dve.tensor_tensor(xt_part(b, j, 1), tr_bank(m), xt_part(b, j, 0), ALU.subtract
                              ).then_inc(xt_lo, 1)

        def mlp_chunk(b, i):
            m = NCH * b + i
            xc = X[:, b * IMG + i * CH:b * IMG + (i + 1) * CH]
            dve.wait_ge(ty_mm, m + 1)
            dve.tensor_tensor(xc, bank(TR_BANK + m % 2), xc, ALU.add).then_inc(x_new, 1)
            dve.wait_ge(x_new, x_new_at[("y", b, i)])
            if i == 0:
                dve.wait_ge(*aggregated(8 + b))
            stats_chunk(12 + b, xc, i)
            bn_count[0] += 1

        def split_low(src, dst, landed, high, made, e):
            dve.wait_ge(landed, 16 * e + 16)
            dve.wait_ge(high, e + 1)
            dve.scalar_tensor_tensor(out=dst[:, 1], in0=src[:], scalar=WS, in1=dst[:, 0],
                                     op0=ALU.mult, op1=ALU.subtract).then_inc(made, 1)

        def zero_pads(s):
            dve.memset(XN[s][:, :, :, 0:PITCH:PITCH - 1], 0.0).then_inc(pads_ok[s], 1)

        def zero_halo(s):
            dve.memset(HALO[s][0:ONES, 0:NT:NT - 1], 0.0).then_inc(halo_ok[s], 1)

        def set_ones(s):
            dve.memset(HALO[s][ONES:KH].bitcast(U32), ONES_BITS).then_inc(halo_ok[s], 1)

        for s in range(2):
            zero_pads(s)
            zero_halo(s)
        set_ones(0)
        dve.memset(MSK[:, 3, 0:2], 0.0).then_inc(msk_ok, 1)
        dve.wait_ge(const_ok, MASKS_MADE)
        dve.tensor_reduce(MSK[:, 0], BAND[:].rearrange("p y c r -> p y r c"), AX_X, ALU.add
                          ).then_inc(msk_ok, 1)
        dve.wait_ge(msk_ok, 2)
        dve.tensor_copy(MSK[:, 1:KX], MSK[:, 0:1].broadcast_to([P, KX - 1, KY, R])
                        ).then_inc(msk_ok, 1)
        dve.tensor_reduce(MSK[:, 3, 0:KY:KY - 1], EDGE[:].rearrange("p h s r -> p s r h"),
                          AX_X, ALU.add).then_inc(msk_ok, 1)
        dve.wait_ge(msk_ok, 4)
        dve.memset(MSK[ONES:KH, 3, 0], 1.0).then_inc(msk_ok, 1)
        input_stats(0, 0, NCH)
        deviation(0)
        variance(0)
        build(0)
        input_stats(1, 0, NCH)
        for g in range(8):
            dve.wait_ge(*aggregated(g))
            if g == 0:
                input_stats(2, 0, 2)
                deviation(1)
                input_stats(2, 2, 3)
                variance(1)
            if g == 1:
                deviation(2)
                input_stats(3, 0, NCH // 2)
                variance(2)
                input_stats(3, NCH // 2, NCH)
            i = 0
            while i < NCH:
                i1 = i + 1
                stops = {SLOTS[n][k] for n in FINISH[g] for k in range(2)} | {3, NCH - 1}
                while i1 < NCH and i1 - 1 not in stops:
                    i1 += 1
                if g == 7 and i == 2:
                    split_low(W1F, W1S, w1_in, w1_hi, w1_ok, 0)
                if g >= 5 and i1 > PREP_AT[g]:
                    for i in range(i, i1):
                        conv_chunk(g, i, i % RING, x_new_at[("c", g, i)])
                        bn_count[0] += 1
                        j = 2 * (i - PREP_AT[g])
                        if 0 <= j < NCH:
                            xt_low(g - 5, j)
                            xt_low(g - 5, j + 1)
                else:
                    conv_chunks(g, i, i1)
                i = i1
                for n in finishing(g, i - 1, 0):
                    if n > 2:
                        deviation(n)
                for n in finishing(g, i - 1, 1):
                    if n > 2:
                        variance(n)
                if g == 0 and i == 4:
                    input_stats(2, 3, NCH)
                if g in (2, 3) and i == 4:
                    build(g - 1)
            aggregate(4 + g)

        def hidden(e, p, extra=None, first=False, high=True):
            if not first:
                dve.wait_ge(g2_mm, e * 4 + (2 * p - 2))
            for ft in range(FT):
                a = e * 16 + (p * FT + ft)
                if high:
                    dve.wait_ge(gelu_ok, a + 1)
                    dve.tensor_scalar(HID[p][:, 0, ft], SCR[:, ft % 2], HS, None, ALU.mult
                                      ).then_inc(hid_hi, 1)
                dve.wait_ge(hid_hi, a + 1)
                dve.scalar_tensor_tensor(out=HID[p][:, 1, ft], in0=SCR[:, ft % 2],
                                         scalar=HS, in1=HID[p][:, 0, ft], op0=ALU.mult,
                                         op1=ALU.subtract).then_inc(hid_ok, 1)
                if extra is not None:
                    extra(ft)

        def next_w1(e):
            split_low(W1F, W1S, w1_in, w1_hi, w1_ok, e)

        def w2_parts(e):
            split_low(W2F, W2S, w2_in, w2_hi, w2_ok, e)

        def in_first(ft):
            if ft == 1:
                deviation(11)
            if ft == 3:
                variance(11)
            if ft == 5:
                w2_parts(0)

        hidden(0, 0, in_first, first=True)
        for j in range(NCH):
            xt_low(3, j)
        dve.wait_ge(pre_mm, NB * NCH)
        hidden(0, 1, first=True)
        next_w1(1)
        with dve.Fori(1, NE - 1) as e:
            w2_parts(e)
            for p in range(NPAIR):
                hidden(e, p)
            next_w1(e + 1)

        e = NE - 1
        w2_parts(e)
        hidden(e, 0)
        dve.wait_ge(w1_ok, NE)
        zero_halo(0)
        dve.wait_ge(w2_ok, NE)
        zero_halo(1)

        def results_of_image_0(ft):
            for i in RESULTS_AT[ft]:
                mlp_chunk(0, i)

        hidden(e, 1, results_of_image_0, high=False)
        aggregate(12)
        deviation(12)
        mlp_chunk(1, 0)
        variance(12)
        dve.wait_ge(g2_mm, 4 * (NE - 1) + 2)
        zero_pads(0)
        for i in range(1, NCH):
            mlp_chunk(1, i)
        aggregate(13)
        dve.wait_ge(g2_mm, 4 * NE)
        zero_pads(1)

        def statistics(g, i):
            for n in finishing(g, i, 0):
                deviation(n)
            for n in finishing(g, i, 1):
                variance(n)

        mlp_chunk(2, 0)
        deviation(13)
        mlp_chunk(2, 1)
        mlp_chunk(2, 2)
        variance(13)
        for i in range(3, NCH):
            mlp_chunk(2, i)
        aggregate(14)
        for i in range(NCH):
            conv_chunk(8, i, i % RING, 0)
            if i > 1:
                statistics(8, i)
        for i in range(NCH):
            if i < NCH // 2:
                mlp_chunk(3, 2 * i)
                mlp_chunk(3, 2 * i + 1)
            conv_chunk(9, i, i % RING, 0)
            if i == NCH // 2 - 1:
                aggregate(15)
            statistics(9, i)
        for g in (10, 11):
            conv_chunks(g, 0, RING)
            conv_chunks(g, RING, NCH)

    @block.tensor
    def _(pe):
        def group_mean(n):
            pe.wait_ge(*aggregated(n))
            if n in (12, 13):
                if n == 12:
                    pe.wait_ge(gelu_ok, NE * NPAIR * FT)
                else:
                    pe.wait_ge(yt_ok, 4 * NE)
            elif n >= 2:
                pe.wait_ge(var_ok, n - 1)
            pe.matmul(stat_psum(n, 0), GRP[:], MV[:, n, 0:1], start=True, stop=True
                      ).then_inc(mean_mm, 1)

        def group_variance(n):
            pe.wait_ge(spread_ok, n + 1)
            pe.matmul(stat_psum(n, 1), GRP[:], SM[:, n, 1:2], start=True, stop=True
                      ).then_inc(var_mm, 1)

        def conv_main(g, i, k):
            s, l = g % 2, g // 4
            pe.wait_ge(hi_ok, i + (NCH * g + 1))
            pe.wait_ge(lo_ok, i + (NCH * g + 1))
            n = 0
            for kx in range(KX):
                for part, w in ((0, 0), (1, 0), (0, 1)):
                    rhs = XN[s][:, part, ds(i * TC, TC), kx:kx + NW]
                    pe.matmul(bank(k), CWT[:, l, w, kx], rhs, start=(n == 0), stop=False)
                    n += 1

        def conv_halo(g, i, k):
            s, l = g % 2, g // 4
            if g == 0 and i * TC < NT // 2:
                pe.wait_ge(halo_first, 64)
            else:
                pe.wait_ge(halo_in[s], 64 * (g // 2 + 1))
            for w in range(2):
                rhs = HALO[s][0:KH, ds(i * TC, TC), 0:NW]
                mm = pe.matmul(bank(k), CWT[0:KH, l, w, 3], rhs, start=False, stop=(w == 1))
            mm.then_inc(conv_mm, 1)

        def conv_chunk(g, i, k):
            conv_main(g, i, k)
            conv_halo(g, i, k)

        def statistics(g, i):
            for n in finishing(g, i, 0):
                group_mean(n)
            for n in finishing(g, i, 1):
                group_variance(n)

        def before_step(g):
            if g % 4 == 0:
                pe.wait_ge(build_ok[g // 4], BUILD_STEPS)
            pe.wait_ge(pads_ok[g % 2], 1 if g < 8 else 2)
            pe.wait_ge(halo_ok[g % 2], 2 if g < 8 else 4)

        def conv_chunks(g, i0, i1):
            before = x_new_at[("c", g + (i0 - RING) // NCH, (i0 - RING) % NCH)]
            with pe.Fori(i0, i1) as i:
                pe.wait_ge(x_new, i + (before - i0))
                conv_chunk(g, i, i - i0 // RING * RING)

        def pre_transposes(b, j):
            m = NCH * b + j
            pe.wait_ge(pre_ok, m + 1)
            if m == 0:
                pe.wait_ge(build_ok[2], BUILD_STEPS)
            if m == 1:
                pe.wait_ge(bt_ok, 1)
            if m >= 2:
                pe.wait_ge(xt_lo, m - 1)
            to = bank(TR_BANK + m % 2)
            for h in range(DH):
                for t in range(TC):
                    mm = pe.transpose(to[:, (h * TC + t) * P:(h * TC + t + 1) * P],
                                      pre(b, j)[:, t * NW + h * P:t * NW + (h + 1) * P], IDF[:])
            mm.then_inc(pre_mm, 1)

        def result_transposes(b, i):
            m = NCH * b + i
            if m < 2:
                pe.wait_ge(xt_lo, NB * NCH)
                pe.wait_ge(yt_ok, 4 * (NE - 1) + 2)
            else:
                pe.wait_ge(x_new, x_new_at[("y", (m - 2) // NCH, (m - 2) % NCH)])
            if b >= 2:
                pe.wait_ge(yt_ok, 4 * NE)
            to = bank(TR_BANK + m % 2)
            for t in range(TC):
                for h in range(DH):
                    tt = (b % 2) * NT + i * TC + t
                    mm = pe.transpose(to[:, t * NW + h * P:t * NW + (h + 1) * P],
                                      YT[:, b // 2, h, tt], IDF[:])
            mm.then_inc(ty_mm, 1)

        def hidden(e, p, between=None):
            for ft in range(FT):
                a = e * 16 + (p * FT + ft)
                if isinstance(e, int) and a < RING:
                    pe.wait_ge(x_new, last_x_new(("c", 7)))
                else:
                    pe.wait_ge(gelu_ok, a - (RING - 1))
                if ft == 0:
                    pe.wait_ge(w1_ok, e + 1)
                    if isinstance(e, int) and e == 0:
                        pe.wait_ge(xt_lo, 2 * NCH * (p + 1))
                n = 0
                for h in range(DH):
                    for part, w in ((0, 0), (1, 0), (0, 1)):
                        mm = pe.matmul(
                            bank(ft % RING),
                            W1S[:, w, h * NF + ft * P:h * NF + (ft + 1) * P],
                            XT[:, p, h, :, e, part], start=(n == 0),
                            stop=(n == 3 * DH - 1))
                        n += 1
                mm.then_inc(g1_mm, 1)
                if between is not None:
                    between(ft)

        def output(e, p, h, between=None):
            k = p * DH + h
            if isinstance(e, int) and 4 * e + k < 2:
                pe.wait_ge(var_ok, 12)
            else:
                pe.wait_ge(yt_ok, e * 4 + (k - 1))
            for ft in range(FT):
                if h == 0:
                    pe.wait_ge(hid_ok, e * 16 + (p * FT + ft + 1))
                if ft == 0 and k == 0:
                    pe.wait_ge(w2_ok, e + 1)
                for part, w in ((0, 0), (1, 0), (0, 1)):
                    mm = pe.matmul(bank(G2_BANK + h),
                                   W2S[:, w, ft * NW + h * P:ft * NW + (h + 1) * P],
                                   HID[p][:, part, ft],
                                   start=(ft == 0 and part == 0 and w == 0),
                                   stop=(ft == FT - 1 and w == 1))
                if between is not None:
                    if ft == FT - 1:
                        mm.then_inc(g2_mm, 1)
                    between(ft)
            if between is None:
                mm.then_inc(g2_mm, 1)

        def expert(e):
            for p in range(NPAIR):
                hidden(e, p)
            for p in range(NPAIR):
                for h in range(DH):
                    output(e, p, h)

        pe.wait_ge(const_ok, SELW_MADE)
        pe.wait_ge(cw_in, 32)
        for k in range(4):
            pe.matmul(TAPS[:, k].rearrange("p l y o -> p (l y o)"), SELW[:, k],
                      WK[:].rearrange("k l y o -> k (l y o)"), start=True, stop=True
                      ).then_inc(taps_mm, 1)
        pe.wait_ge(const_ok, CONSTS_MADE)
        pe.wait_ge(bb_in, 32)
        nb = (FT + DH) * NE
        pe.transpose(bank(TR_BANK + 1)[:, 0:nb], BB[:], IDF[0:nb, 0:nb]).then_inc(bt_mm, 1)
        group_mean(0)
        group_variance(0)
        for g in range(2):
            before_step(g)
            for i in range(RING):
                if g > 0:
                    pe.wait_ge(x_new, x_new_at[("c", g - 1, i + RING)])
                conv_main(g, i, i)
                statistics(g, i)
            for i in range(RING):
                conv_halo(g, i, i)
            for i in range(RING, NCH):
                pe.wait_ge(x_new, x_new_at[("c", g, i - RING)])
                conv_chunk(g, i, i - RING)
                statistics(g, i)
        for g in range(2, 8):
            before_step(g)
            if g < 5:
                stops = sorted({SLOTS[n][k] + 1 for n in FINISH[g] for k in range(2)} | {RING, NCH})
                for i0, i1 in zip([0] + stops, stops):
                    conv_chunks(g, i0, i1)
                    statistics(g, i1 - 1)
            else:
                for i in range(NCH):
                    pe.wait_ge(x_new, x_new_at[("c", g + (i - RING) // NCH, (i - RING) % NCH)])
                    conv_chunk(g, i, i % RING)
                    statistics(g, i)
                    j = 2 * (i - PREP_AT[g])
                    if 0 <= j < NCH:
                        pre_transposes(g - 5, j)
                        pre_transposes(g - 5, j + 1)

        def in_first_hidden(ft):
            if ft == 1:
                group_mean(11)
            if ft == 3:
                group_variance(11)

        hidden(0, 0, in_first_hidden)
        for h in range(DH):
            output(0, 0, h, lambda ft: pre_transposes(3, h * FT // 2 + ft // 2) if ft % 2 else None)
        hidden(0, 1)
        for h in range(DH):
            output(0, 1, h)
        with pe.Fori(1, NE - 1) as e:
            expert(e)
        e = NE - 1
        hidden(e, 0)
        for h in range(DH):
            output(e, 0, h)

        def results_of_image_0(ft):
            for i in RESULTS_AT[ft]:
                result_transposes(0, i)

        def in_output_0(ft):
            if ft == 3:
                group_mean(12)
            if ft == 4:
                result_transposes(1, 0)
            if ft == 5:
                group_variance(12)
            if ft >= 6:
                result_transposes(1, ft - 5)

        def in_output_1(ft):
            if ft in (1, 2, 4, 5, 7):
                result_transposes(1, 3 + (1, 2, 4, 5, 7).index(ft))

        hidden(e, 1, results_of_image_0)
        output(e, 1, 0, in_output_0)
        output(e, 1, 1, in_output_1)

        before_step(8)
        for i in range(RING):
            result_transposes(2, 2 * i)
            result_transposes(2, 2 * i + 1)
            if i == 0:
                pe.wait_ge(gelu_ok, NE * NPAIR * FT)
                pe.wait_ge(var_ok, 13)
            conv_main(8, i, i)
            statistics(8, i)
        for i in range(RING):
            conv_halo(8, i, i)
        for i in range(RING, NCH):
            pe.wait_ge(x_new, x_new_at[("c", 8, i - RING)])
            conv_chunk(8, i, i - RING)
            statistics(8, i)
        before_step(9)
        for i in range(NCH):
            if i < NCH // 2:
                result_transposes(3, 2 * i)
                result_transposes(3, 2 * i + 1)
            pe.wait_ge(x_new, x_new_at[("c", 9 + (i - RING) // NCH, (i - RING) % NCH)])
            conv_chunk(9, i, i % RING)
            statistics(9, i)
        for g in (10, 11):
            before_step(g)
            conv_chunks(g, 0, RING)
            conv_chunks(g, RING, NCH)

    ctx.close()


CONVS = ("L0", "L1", "L3")
DENSE = ("L2_conv_w1", "L2_conv_b1", "L2_conv_w2", "L2_conv_b2")


def kernel(**inputs):
    import concourse.bacc as bacc
    import numpy as np
    from concourse.bass_utils import run_bass_kernel_spmd

    nc = bacc.Bacc("TRN2", target_bir_lowering=False, num_devices=1)
    arrays = {name: np.asarray(inputs[name]) for name in ("x",) + DENSE}
    weights = np.stack([np.asarray(inputs[f"{l}_conv_weight"]) for l in CONVS])
    arrays["conv_weights"] = weights.transpose(2, 4, 0, 3, 1)
    arrays["conv_biases"] = np.stack([np.asarray(inputs[f"{l}_conv_bias"]) for l in CONVS])
    arrays = {name: np.ascontiguousarray(a) for name, a in arrays.items()}
    t = {name: nc.dram_tensor(name, a.shape, F32, kind="ExternalInput").ap()
         for name, a in arrays.items()}
    out = nc.dram_tensor("out", (NB, NC, NH, NW), F32, kind="ExternalOutput").ap()
    bass_program(nc, t["x"], t["conv_weights"], t["conv_biases"], *(t[n] for n in DENSE), out)
    return run_bass_kernel_spmd(nc, [arrays], core_ids=[0]).results[0]["out"]
```

```python
from contextlib import ExitStack

import concourse.bass as bass
from concourse import mybir

ALU = mybir.AluOpType
ACT = mybir.ActivationFunctionType
F32 = mybir.dt.float32
F16 = mybir.dt.float16
U32 = mybir.dt.uint32
AX_X = mybir.AxisListType.X
ds = bass.ds

P = 128
NB, NC, NH, NW = 4, 8, 256, 256
R = P // NC
NT = NH // R
IMG = NT * NW
CH = 512
NCH = IMG // CH
TC = CH // NW
PITCH = NW + 2
GROUP = 2 * R
EPS = 1e-5
NE, NF = 8, 1024
FT = NF // P
DH = NW // P
NPAIR = NB // 2
TT = 2 * NT
KX = KY = 3
HROWS = 2 * NC * KX
ONES = 2 * HROWS
KH = ONES + 1
XS, WS, HS = 64.0, 256.0, 16.0

STAT_AT = {1: ((0, 2), (0, 3)), 2: ((0, 6), (0, 7)), 3: ((1, 3), (1, 4)),
           4: ((2, 2), (2, 3)), 5: ((2, 4), (2, 5)), 6: ((3, 3), (3, 5)), 7: ((4, 3), (4, 5)),
           8: ((5, 0), (5, 1)), 9: ((6, 0), (6, 1)), 10: ((7, 0), (7, 1)),
           13: ((8, 0), (8, 1)), 14: ((8, 6), (8, 7)), 15: ((9, 6), (9, 7))}
PREP_AT = {5: 5, 6: 5, 7: 3}


def finishing(g, i, second):
    return [n for n, at in STAT_AT.items() if at[second] == (g, i)]


def statistics_stops(g):
    return {at[k][1] for at in STAT_AT.values() for k in range(2) if at[k][0] == g}


def prepared_after(g, i):
    if g > 5 and i == 0:
        return [(g - 6, NCH - 2), (g - 6, NCH - 1)]
    j = 2 * (i - PREP_AT[g])
    return [(g - 5, j), (g - 5, j + 1)] if 0 <= j < NCH else []


def stat_of_step(g):
    return g if g < 8 else g + 4


def image_of_step(g):
    return g % 4


FIRST_TILES = 12
HALO_TILES, HALO_CHUNKS = 6, 4
LATE_HALO = ([("main", i) for i in range(4)] + [("halo", i) for i in range(3)]
             + [("main", i) for i in range(4, 7)] + [("halo", i) for i in range(3, 7)]
             + [("main", 7), ("halo", 7)])
WARM_UP = 8
RSTD_STEPS = 3
WROWS = NC * KX + 1


def bass_program(nc, x, cw, cb, w1, b1, w2, b2, out):
    ctx = ExitStack()

    def at(name, offset, shape, dt):
        return nc.alloc_sbuf_tensor_at(name, shape, dt, offset=offset)

    def sem(name):
        return nc.alloc_semaphore(name)

    base = (nc.sbuf_base + 31) // 32 * 32
    X_OFF = base
    XY_OFF = X_OFF + NB * IMG * 4
    XN_OFF = XY_OFF + NB * IMG * 4
    XN_SLOT = 2 * NT * PITCH * 2
    HALO_OFF = XN_OFF + 2 * XN_SLOT
    HALO_SLOT = NT * PITCH * 2
    W1S_OFF = HALO_OFF + 2 * HALO_SLOT
    W2S_OFF = W1S_OFF + 2 * DH * NF * 2
    CW_OFF = W2S_OFF + 2 * FT * NW * 2
    SCR_OFF = CW_OFF + 3 * 2 * 4 * P * 2
    C_OFF = SCR_OFF + 2 * CH * 4

    X = at("X", X_OFF, [P, NB * IMG], F32)
    XT = at("XT", XY_OFF, [P, NPAIR, DH, TT, NC, 2, R], F16)
    YT = at("YT", XY_OFF, [P, NPAIR, DH, TT, NC * R], F32)
    XN = [at(f"XN{s}", XN_OFF + s * XN_SLOT, [P, 2, NT, PITCH], F16) for s in range(2)]
    HALO = [at(f"HALO{s}", HALO_OFF + s * HALO_SLOT, [P, NT, PITCH], F16) for s in range(2)]
    HID = [at(f"HID{p}", XN_OFF + p * XN_SLOT, [P, 2, FT, CH], F16) for p in range(NPAIR)]
    W1F = at("W1F", HALO_OFF, [P, DH * NF], F32)
    W2F = at("W2F", HALO_OFF + HALO_SLOT, [P, FT * NW], F32)
    W1S = at("W1S", W1S_OFF, [P, 2, DH * NF], F16)
    W2S = at("W2S", W2S_OFF, [P, 2, FT * NW], F16)
    PRE = at("PRE", W2S_OFF, [P, 4, CH], F32)
    PRE3 = at("PRE3", XN_OFF + XN_SLOT, [P, NCH, CH], F32)
    CWT = at("CWT", CW_OFF, [P, 3, 2, 4, P], F16)
    SCR = at("SCR", SCR_OFF, [P, 2, CH], F32)
    o = C_OFF
    IDF = at("IDF", o, [P, P], F32); o += P * 4
    GRP = at("GRP", o, [P, P], F32); o += P * 4
    BT = at("BT", o, [P, (FT + DH) * NE], F32); o += (FT + DH) * NE * 4
    ST = at("ST", o, [P, 4, NCH, 6], F32); o += 4 * NCH * 6 * 4
    MV = at("MV", o, [P, 16, 2], F32); o += 16 * 2 * 4
    SM = at("SM", o, [P, 16, 5], F32); o += 16 * 5 * 4
    SC = at("SC", o, [P, 16, 2], F32); o += 16 * 2 * 4
    RS = at("RS", o, [P, 8], F32); o += 32
    HALF = RS[:, 2:3]
    assert o <= nc.sbuf_usable_end, (o, nc.sbuf_usable_end)
    s0 = XY_OFF
    WK = at("WK", s0, [WROWS, 3, KY, NC], F32); s0 += 3 * KY * NC * 4
    SELW = at("SELW", s0, [WROWS, 4, P], F32); s0 += 4 * P * 4
    BLK = at("BLK", s0, [P, NC, R], F32); s0 += P * 4
    BAND = at("BAND", s0, [P, KY, NC, R], F32); s0 += NC * KY * R * 4
    EDGE = at("EDGE", s0, [P, 2, 2, R], F32); s0 += 4 * R * 4
    MSK = at("MSK", s0, [P, 4, KY, R], F32); s0 += 4 * KY * R * 4
    ACC = at("ACC", s0, [P, 4, NC, R], F32); s0 += 4 * P * 4
    TMP = at("TMP", s0, [P, 4, NC, R], F32); s0 += 4 * P * 4
    BB = at("BB", s0, [(FT + DH) * NE, P], F32)

    PS = nc.alloc_psum_tensor("PS", [P, 8 * CH], F32)
    RING, G2_BANK, TR_BANK = 4, 4, 6

    def bank(k):
        return PS[:, ds(k * CH, CH)] if not isinstance(k, int) else PS[:, k * CH:(k + 1) * CH]

    def stat_psum(n, col):
        k = 0 if n == 12 else G2_BANK + n % 2
        return PS[:, k * CH + col:k * CH + col + 1]

    TAPS = PS[:, TR_BANK * CH:TR_BANK * CH + 4 * 3 * KY * NC].rearrange(
        "p (m l y o) -> p m l y o", m=4, l=3, y=KY)

    def tr_bank(m):
        return bank(TR_BANK + m % 2).rearrange("p (h t c r) -> p h (t c) r", h=DH, t=TC, c=NC)

    def pre(b, j):
        return PRE[:, j % 4] if b < NB - 1 else PRE3[:, j]

    def xt_part(b, j, h):
        tt = (b % 2) * NT + j * TC
        return XT[:, b // 2, :, tt:tt + TC, :, h, :].rearrange("p h t c r -> p h (t c) r")

    def yt_part(e, p, dh):
        return YT[:, p, dh, :, ds(e * R, R)]

    x0_in = [sem(f"x0_in{i}") for i in range(2)]
    x_in = {b: sem(f"x_in{b}") for b in range(1, NB)}
    cw_in = sem("cw_in")
    bb_in = sem("bb_in")
    halo_first = sem("halo_first")
    halo_in = [sem(f"halo_in{s}") for s in range(2)]
    w1_in, w2_in = sem("w1_in"), sem("w2_in")
    out_done = sem("out_done")
    const_ok = sem("const_ok")
    wk_zero = sem("wk_zero")
    msk_ok = sem("msk_ok")
    taps_mm = sem("taps_mm")
    pads_ok = [sem(f"pads_ok{s}") for s in range(2)]
    halo_ok = [sem(f"halo_ok{s}") for s in range(2)]
    build_ok = [sem(f"build_ok{l}") for l in range(3)]
    bt_mm, bt_ok = sem("bt_mm"), sem("bt_ok")
    bn_ok = sem("bn_ok")
    mv_in = sem("mv_in")
    mv_ok = sem("mv_ok")
    mean_mm = sem("mean_mm")
    dev_ok = sem("dev_ok")
    spread_ok = sem("spread_ok")
    var_mm = sem("var_mm")
    var_ok = sem("var_ok")
    rstd_ok = sem("rstd_ok")
    half_ok = sem("half_ok")
    norm_ok = sem("norm_ok")
    xn_ok = sem("xn_ok")
    hi_ok = sem("hi_ok")
    lo_ok = sem("lo_ok")
    conv_mm = sem("conv_mm")
    x_new = sem("x_new")
    pre_ok = sem("pre_ok")
    pre_mm = sem("pre_mm")
    xt_hi = sem("xt_hi")
    xt_lo = sem("xt_lo")
    w1_hi, w1_ok = sem("w1_hi"), sem("w1_ok")
    w2_hi, w2_ok = sem("w2_hi"), sem("w2_ok")
    g1_mm = sem("g1_mm")
    gelu_ok = sem("gelu_ok")
    hid_hi, hid_ok = sem("hid_hi"), sem("hid_ok")
    g2_mm = sem("g2_mm")
    yt_ok = sem("yt_ok")
    ty_mm = sem("ty_mm")

    block = ctx.enter_context(nc.Block())

    order = [("c", g, i) for g in range(8) for i in range(NCH)]
    order += [("y", b, i) for b in range(2) for i in range(NCH)]
    order += [("y", 2, i) for i in range(6)] + [("c", 8, i) for i in range(RING)]
    order += [("y", 2, i) for i in (6, 7)] + [("c", 8, i) for i in range(RING, NCH)]
    for i in range(NCH):
        order += [("y", 3, 2 * i + k) for k in range(2) if i < NCH // 2] + [("c", 9, i)]
    order += [("c", g, i) for g in (10, 11) for i in range(NCH)]
    x_new_at = {k: n + 1 for n, k in enumerate(order)}

    def aggregated(n):
        return (mv_in, n + 1) if n < NB else (mv_ok, n - NB + 1)

    def last_x_new(key):
        return x_new_at[(key[0], key[1], NCH - 1)]

    @block.sync
    def _(sp):
        def move_image(b, t0, t1, store, signal):
            for c in range(NC):
                sb = X[c * R:(c + 1) * R, b * IMG + t0 * NW:b * IMG + t1 * NW]
                sb = sb.rearrange("r (t w) -> r t w", w=NW)
                dr = (out if store else x)[b, c].rearrange("(t r) w -> r t w", r=R)[:, t0:t1]
                sp.dma_start(dr if store else sb, sb if store else dr).then_inc(signal, 16)

        def move_tile(b, t, store, signal):
            sb = X[:, b * IMG + t * NW:b * IMG + (t + 1) * NW]
            dr = (out if store else x)[b, :, t * R:(t + 1) * R]
            sp.dma_start(dr if store else sb, sb if store else dr).then_inc(signal, 16)

        move_image(0, 0, FIRST_TILES, False, x0_in[0])
        move_image(0, FIRST_TILES, NT, False, x0_in[1])
        for b in (1, 2):
            move_image(b, 0, NT, False, x_in[b])

        def shifted_rows(s, h, side, t0, nt, signal):
            run = (nt - 1) * PITCH + NW
            src = XN[s][(R - 1) * (1 - side):P:R, h, t0 - 1 + 2 * side:]
            src = src.rearrange("p t w -> p (t w)")
            src = bass.AP(src.tensor, src.offset, [src.ap[0], (1, KX), (1, run)])
            dst = HALO[s][:].rearrange("p t w -> p (t w)")
            row = h * HROWS + side * NC * KX
            sp.dma_start(dst[row:row + NC * KX, t0 * PITCH:t0 * PITCH + run], src
                         ).then_inc(signal, 16)

        def halos(g):
            s = g % 2
            if g >= 2:
                sp.wait_ge(conv_mm, NCH * (g - 1))
            sp.wait_ge(pads_ok[s], 1 if g < 8 else 2)
            sp.wait_ge(halo_ok[s], 2 if g < 8 else 4)
            if g == 0:
                for h in range(2):
                    sp.wait_ge(hi_ok if h == 0 else lo_ok, HALO_CHUNKS)
                    shifted_rows(s, h, 0, 1, HALO_TILES - 1, halo_first)
                    shifted_rows(s, h, 1, 0, HALO_TILES, halo_first)
            for h in range(2):
                sp.wait_ge(hi_ok if h == 0 else lo_ok, NCH * (g + 1))
                for side in range(2):
                    t0 = HALO_TILES if g == 0 else 1 - side
                    t1 = NT - side
                    shifted_rows(s, h, side, t0, t1 - t0, halo_in[s])

        def load_w1(e):
            if e > 0:
                sp.wait_ge(w1_ok, e)
            sp.dma_start(W1F[:].rearrange("p (h f) -> p h f", h=DH),
                         w1[e].rearrange("(h p) f -> p h f", p=P)).then_inc(w1_in, 16)

        def load_w2(e):
            if e > 0:
                sp.wait_ge(w2_ok, e)
            sp.dma_start(W2F[:].rearrange("p (h d) -> p h d", h=FT),
                         w2[e].rearrange("(h p) d -> p h d", p=P)).then_inc(w2_in, 16)

        for g in range(8):
            halos(g)
            if g == 0:
                move_image(3, 0, NT, False, x_in[3])
        sp.wait_ge(conv_mm, NCH * 7)
        load_w1(0)
        sp.wait_ge(conv_mm, NCH * 8)
        load_w2(0)
        for e in range(1, NE):
            load_w1(e)
            load_w2(e)
        for g in range(8, 12):
            halos(g)
            if g >= 9:
                sp.wait_ge(x_new, last_x_new(("c", g - 1)))
                move_image(g - 9, 0, NT, True, out_done)
        for i in range(NCH):
            sp.wait_ge(x_new, x_new_at[("c", 11, i)])
            for t in range(TC * i, TC * (i + 1)):
                move_tile(NB - 1, t, True, out_done)
        sp.wait_ge(out_done, 16 * (NC * (NB - 1) + NT))

    SELW_MADE, MASKS_MADE, CONSTS_MADE = 8, 16, 19
    ONES_BITS = 0x54005400
    BUILD_STEPS = 2 * KY + 1

    @block.gpsimd
    def _(pool):
        def set_ones(s):
            pool.memset(HALO[s][ONES:KH].bitcast(U32), ONES_BITS).then_inc(halo_ok[s], 1)

        pool.memset(HALF, -0.5).then_inc(half_ok, 1)
        pool.memset(WK[:], 0.0).then_inc(wk_zero, 1)
        pool.memset(SELW[:], 0.0).then_inc(const_ok, 1)
        pool.memset(BLK[:], 1.0).then_inc(const_ok, 1)
        pool.memset(EDGE[:], 1.0).then_inc(const_ok, 1)
        pool.memset(GRP[:], 1.0 / GROUP).then_inc(const_ok, 1)
        pool.memset(IDF[:], 0.0).then_inc(const_ok, 1)
        made = [5]

        def select(into, pattern, base, mult, op, fill, src=None):
            pool.wait_ge(const_ok, made[0])
            pool.affine_select(out=into, in_=into if src is None else src, compare_op=op,
                               fill=fill, base=base, pattern=pattern, channel_multiplier=mult
                               ).then_inc(const_ok, 1)
            made[0] += 1

        select(SELW[:, 0:KX].rearrange("k x (c r) -> k x c r", r=R),
               [[-1, KX], [-KX, NC], [0, R]], 0, 1, ALU.not_equal, 1.0)
        select(SELW[:, 3, 0:ONES].rearrange("k (h j) -> k h j", j=NC * KX),
               [[0, 4], [-1, NC * KX]], 0, 1, ALU.not_equal, 1.0)
        select(SELW[:, 3, ONES:KH], [[0, 1]], -NC * KX, 1, ALU.not_equal, 1.0)
        select(BLK[:], [[-R, NC], [0, R]], 0, 1, ALU.is_ge, 0.0)
        select(BLK[:], [[R, NC], [0, R]], R - 1, -1, ALU.is_ge, 0.0)
        for ky in range(KY):
            select(BAND[:, ky], [[-R, NC], [-1, R]], 1 - ky, 1, ALU.is_equal, 0.0, BLK[:])
        select(EDGE[:], [[-HROWS, 2], [-NC * KX, 2], [0, R]], 0, 1, ALU.is_ge, 0.0)
        select(EDGE[:], [[HROWS, 2], [NC * KX, 2], [0, R]], NC * KX - 1, -1, ALU.is_ge, 0.0)
        select(EDGE[:], [[0, 2], [-(R - 1), 2], [1, R]], 0, 0, ALU.is_equal, 0.0)
        masks_made = made[0]
        grp = GRP[:].rearrange("p (g k) -> p g k", k=GROUP)
        select(grp, [[-GROUP, P // GROUP], [0, GROUP]], 0, 1, ALU.is_ge, 0.0)
        select(grp, [[GROUP, P // GROUP], [0, GROUP]], GROUP - 1, -1, ALU.is_ge, 0.0)
        select(IDF[:], [[-1, P]], 0, 1, ALU.not_equal, 1.0)
        assert (masks_made, made[0]) == (MASKS_MADE, CONSTS_MADE)
        pool.wait_ge(const_ok, CONSTS_MADE)
        set_ones(1)
        pool.wait_ge(halo_ok[1], 2)
        pool.wait_ge(half_ok, 1)

        def scale_and_bias(n):
            pool.wait_ge(var_ok, 2 * (n + 1))
            r0, t = RS[:, 0:1], RS[:, 1:2]
            pool.tensor_tensor(r0, SM[:, n, 2:3], HALF, ALU.pow).then_inc(rstd_ok, 1)
            pool.wait_ge(rstd_ok, RSTD_STEPS * n + 1)
            pool.tensor_scalar(t, r0, r0, SM[:, n, 4:5], ALU.mult, ALU.mult).then_inc(rstd_ok, 1)
            pool.wait_ge(rstd_ok, RSTD_STEPS * n + 2)
            pool.tensor_scalar(SC[:, n, 0:1], t, 1.5 * XS, r0, ALU.add, ALU.mult
                               ).then_inc(rstd_ok, 1)
            pool.wait_ge(rstd_ok, RSTD_STEPS * n + 3)
            pool.tensor_tensor(SC[:, n, 1:2], SM[:, n, 3:4], SC[:, n, 0:1], ALU.mult
                               ).then_inc(norm_ok, 1)

        def low_parts(g, i0=0, i1=NCH // 2):
            q = NCH * g
            with pool.Fori(i0, i1) as i:
                for k in range(2):
                    pool.wait_ge(xn_ok, i * 2 + (q + k + 1))
                    pool.wait_ge(hi_ok, i * 2 + (q + k + 1))
                    rows = ds(i * 2 * TC + k * TC, TC)
                    pool.tensor_tensor(
                        XN[g % 2][:, 1, rows, 1:NW + 1],
                        SCR[:, k].rearrange("p (t w) -> p t w", w=NW),
                        XN[g % 2][:, 0, rows, 1:NW + 1], ALU.subtract).then_inc(lo_ok, 1)

        scale_and_bias(0)
        low_parts(0, 0, 3)
        scale_and_bias(1)
        low_parts(0, 3)
        low_parts(1, 0, 3)
        scale_and_bias(2)
        low_parts(1, 3)
        low_parts(2)
        scale_and_bias(3)
        low_parts(3, 0, 3)
        scale_and_bias(4)
        low_parts(3, 3)
        scale_and_bias(5)
        for g in (3, 4):
            low_parts(g + 1)
            scale_and_bias(g + 3)
        for g in (5, 6):
            low_parts(g + 1, 0, NCH // 4)
            scale_and_bias(g + 3)
            low_parts(g + 1, NCH // 4)
        scale_and_bias(10)
        scale_and_bias(11)
        pool.wait_ge(norm_ok, 12)
        pool.wait_ge(w1_ok, NE)
        set_ones(0)
        pool.wait_ge(halo_ok[0], 4)
        pool.wait_ge(w2_ok, NE)
        set_ones(1)
        pool.wait_ge(halo_ok[1], 4)
        scale_and_bias(12)
        low_parts(8)
        scale_and_bias(13)
        low_parts(9)
        scale_and_bias(14)
        low_parts(10)
        scale_and_bias(15)
        low_parts(11)

    @block.scalar
    def _(act):
        act.wait_ge(wk_zero, 1)
        act.dma_start(WK[0:WROWS - 1], cw.rearrange("c x l y o -> (c x) l y o")
                      ).then_inc(cw_in, 16)
        act.dma_start(WK[WROWS - 1:WROWS, :, 0], cb.unsqueeze(0)).then_inc(cw_in, 16)
        act.wait_ge(x0_in[0], 16 * NC)
        act.dma_start(BB[0:FT * NE], b1.rearrange("e (t p) -> (e t) p", p=P)
                      ).then_inc(bb_in, 16)
        act.dma_start(BB[FT * NE:(FT + DH) * NE], b2.rearrange("e (t p) -> (e t) p", p=P)
                      ).then_inc(bb_in, 16)

        def normalise(g, i0=0, i1=NCH // 2):
            n, b, q = stat_of_step(g), image_of_step(g), NCH * g
            if i0 == 0:
                act.wait_ge(norm_ok, n + 1)
                if g >= 2:
                    act.wait_ge(conv_mm, NCH * (g - 1))
                if g == 8:
                    act.wait_ge(hid_ok, NE * NPAIR * FT)
                if g in (8, 9):
                    act.wait_ge(g2_mm, 4 * (NE - 1) + 2 * (g - 7))

            def whole(i, k):
                act.activation(SCR[:, k], X[:, ds(i * 2 * CH + (b * IMG + k * CH), CH)],
                               ACT.Identity, bias=SC[:, n, 1:2], scale=SC[:, n, 0:1]
                               ).then_inc(xn_ok, 1)

            def high(i, k):
                src = X[:, ds(i * 2 * CH + (b * IMG + k * CH), CH)]
                act.activation(XN[g % 2][:, 0, ds(i * 2 * TC + k * TC, TC), 1:NW + 1],
                               src.rearrange("p (t w) -> p t w", w=NW), ACT.Identity,
                               bias=SC[:, n, 1:2], scale=SC[:, n, 0:1]).then_inc(hi_ok, 1)

            if g == 0:
                for k in range(2):
                    high(0, k)
                    whole(0, k)
                i0 = 1
            with act.Fori(i0, i1) as i:
                for k in range(2):
                    act.wait_ge(lo_ok, i * 2 + (q + k - 1))
                    whole(i, k)
                    high(i, k)

        def pre_chunk(b, j):
            m = NCH * b + j
            if j == 0:
                act.wait_ge(norm_ok, 8 + b + 1)
            if b < NB - 1:
                if m >= 4:
                    act.wait_ge(pre_mm, m - 3)
            elif j == 0:
                act.wait_ge(conv_mm, NCH * 8)
            act.activation(pre(b, j), X[:, b * IMG + j * CH:b * IMG + (j + 1) * CH],
                           ACT.Identity, bias=SC[:, 8 + b, 1:2], scale=SC[:, 8 + b, 0:1]
                           ).then_inc(pre_ok, 1)

        def xt_high(b, j):
            m = NCH * b + j
            act.wait_ge(pre_mm, m + 1)
            act.copy(xt_part(b, j, 0), tr_bank(m)).then_inc(xt_hi, 1)

        def split_high(src, dst, landed, made, e):
            act.wait_ge(landed, 16 * e + 16)
            act.activation(dst[:, 0], src[:], ACT.Copy, scale=WS).then_inc(made, 1)

        def gelu(e, ft, a):
            act.wait_ge(g1_mm, a + 1)
            act.activation(SCR[:, ft % 2], bank(ft % RING), ACT.Gelu,
                           bias=BT[:, ds(e * FT + ft, 1)], scale=1.0 / (XS * WS)
                           ).then_inc(gelu_ok, 1)

        def first_hidden():
            for ft in range(FT):
                if ft == 0:
                    act.wait_ge(lo_ok, NCH * 8)
                elif ft >= 2:
                    act.wait_ge(hid_ok, ft - 1)
                gelu(0, ft, ft)
                if ft == 3:
                    act.wait_ge(pre_mm, (NB - 1) * NCH)
                    split_high(W2F, W2S, w2_in, w2_hi, 0)
                if ft == 5:
                    for j in range(3):
                        pre_chunk(3, j)

        def last_hidden(e):
            for ft in range(FT):
                a = e * 16 + FT + ft
                act.wait_ge(hid_ok, a - 1)
                gelu(e, ft, a)
                act.wait_ge(gelu_ok, a + 1)
                act.activation(HID[1][:, 0, ft], SCR[:, ft % 2], ACT.Copy, scale=HS
                               ).then_inc(hid_hi, 1)

        def hidden(e, p):
            for ft in range(FT):
                act.wait_ge(hid_ok, e * 16 + p * FT + (ft - 1))
                gelu(e, ft, e * 16 + p * FT + ft)

        def next_w1(e):
            act.wait_ge(g1_mm, e * 16)
            split_high(W1F, W1S, w1_in, w1_hi, e)

        def result(e, p, dh):
            act.wait_ge(g2_mm, e * 4 + (p * DH + dh + 1))
            act.activation(
                yt_part(e, p, dh),
                bank(G2_BANK + dh).rearrange("p (t r) -> p t r", r=R),
                ACT.Identity, bias=BT[:, ds(e * DH + (NE * FT + dh), 1)],
                scale=1.0 / (HS * WS)).then_inc(yt_ok, 1)

        def results(e):
            for p in range(NPAIR):
                for dh in range(DH):
                    result(e, p, dh)

        normalise(0)
        act.wait_ge(bt_mm, 1)
        act.copy(BT[:], bank(TR_BANK + 1)[:, 0:(FT + DH) * NE]).then_inc(bt_ok, 1)
        for g in range(5):
            normalise(g + 1)
        for g in (5, 6):
            b = g - 5
            normalise(g + 1, 0, 1)
            if b > 0:
                xt_high(b - 1, 6)
                xt_high(b - 1, 7)
            normalise(g + 1, 1)
            for j in range(4):
                pre_chunk(b, j)
            for j in range(0, 6, 2):
                xt_high(b, j)
                xt_high(b, j + 1)
                if j < 4:
                    pre_chunk(b, j + 4)
                    pre_chunk(b, j + 5)
        xt_high(1, 6)
        xt_high(1, 7)
        split_high(W1F, W1S, w1_in, w1_hi, 0)
        for j in range(NCH + 2):
            if j < NCH:
                pre_chunk(2, j)
            if j >= 2:
                xt_high(2, j - 2)
        act.wait_ge(half_ok, 1)
        act.activation(RS[:, 3:4], HALF, ACT.Gelu)
        act.wait_ge(bt_ok, 1)
        first_hidden()
        for j in range(NCH):
            if j < NCH - 3:
                pre_chunk(3, j + 3)
            xt_high(3, j)
            if j == NCH // 2:
                result(0, 0, 0)
        result(0, 0, 1)
        hidden(0, 1)
        next_w1(1)
        result(0, 1, 0)
        result(0, 1, 1)

        def expert(e):
            act.wait_ge(g2_mm, e * 4)
            split_high(W2F, W2S, w2_in, w2_hi, e)
            with act.Fori(0, NPAIR) as p:
                hidden(e, p)

        with act.Fori(1, NE - 1) as e:
            expert(e)
            next_w1(e + 1)
            results(e)
        e = NE - 1
        act.wait_ge(g2_mm, e * 4)
        split_high(W2F, W2S, w2_in, w2_hi, e)
        hidden(e, 0)
        result(e, 0, 0)
        result(e, 0, 1)
        last_hidden(e)
        normalise(8, 0, 1)
        result(e, 1, 0)
        normalise(8, 1, 2)
        result(e, 1, 1)
        normalise(8, 2)
        for g in range(9, 12):
            normalise(g)

    @block.vector
    def _(dve):
        bn_count = [0]

        def stats_chunk(n, src, slot):
            dve.bn_stats(ST[:, n % 4, slot], src).then_inc(bn_ok, 1)

        def aggregate(n):
            dve.wait_ge(bn_ok, bn_count[0])
            dve.bn_aggr(MV[:, n], ST[:, n % 4].rearrange("p c s -> p (c s)")
                        ).then_inc(aggregated(n)[0], 1)

        def deviation(n):
            dve.wait_ge(mean_mm, n + 1)
            mean = stat_psum(n, 0)
            dve.tensor_tensor(SM[:, n, 0:1], MV[:, n, 0:1], mean, ALU.subtract
                              ).then_inc(dev_ok, 1)
            dve.tensor_scalar(SM[:, n, 3:4], mean, -1.0, None, ALU.mult).then_inc(dev_ok, 1)
            dve.wait_ge(dev_ok, 2 * n + 2)
            dve.scalar_tensor_tensor(out=SM[:, n, 1:2], in0=SM[:, n, 0:1],
                                     scalar=SM[:, n, 0:1], in1=MV[:, n, 1:2],
                                     op0=ALU.mult, op1=ALU.add).then_inc(spread_ok, 1)

        def variance(n):
            dve.wait_ge(var_mm, n + 1)
            dve.tensor_scalar(SM[:, n, 2:3], stat_psum(n, 1), EPS, None, ALU.add
                              ).then_inc(var_ok, 1)
            dve.tensor_scalar(SM[:, n, 4:5], stat_psum(n, 1), EPS, -0.5 * XS, ALU.add, ALU.mult
                              ).then_inc(var_ok, 1)

        def input_stats(b, i0, i1):
            for i in range(i0, i1):
                if b == 0:
                    dve.wait_ge(x0_in[i * TC // FIRST_TILES], 16 * NC)
                else:
                    dve.wait_ge(x_in[b], 16 * NC)
                stats_chunk(b, X[:, b * IMG + i * CH:b * IMG + (i + 1) * CH], i)
            bn_count[0] += i1 - i0
            if i1 == NCH:
                aggregate(b)

        def build_step(l, count, ins):
            ins.then_inc(build_ok[l], 1)
            dve.wait_ge(build_ok[l], count)

        def build_product(l, ky):
            if l > 0 and ky == 0:
                dve.wait_ge(build_ok[l - 1], BUILD_STEPS)
            if l == 0 and ky == 0:
                dve.wait_ge(taps_mm, 4)
                dve.wait_ge(msk_ok, 5)
            weight = TAPS[:, :, l, ky].unsqueeze(3).broadcast_to([P, 4, NC, R])
            mask = MSK[:, :, ky].unsqueeze(2).broadcast_to([P, 4, NC, R])
            into = ACC if ky == 0 else TMP
            build_step(l, 2 * ky + (ky == 0), dve.tensor_tensor(into[:], weight, mask, ALU.mult))
            if ky > 0:
                build_step(l, 2 * ky + 1, dve.tensor_tensor(ACC[:], ACC[:], TMP[:], ALU.add))

        def build_products(l):
            for ky in range(KY):
                build_product(l, ky)

        def build_parts(l):
            acc = ACC[:].rearrange("p s c r -> p (s c r)")
            hi = CWT[:, l, 0].rearrange("p s m -> p (s m)")
            lo = CWT[:, l, 1].rearrange("p s m -> p (s m)")
            build_step(l, 2 * KY, dve.tensor_scalar(hi, acc, WS, None, ALU.mult))
            build_step(l, 2 * KY + 1,
                       dve.scalar_tensor_tensor(out=lo, in0=acc, scalar=WS, in1=hi,
                                                op0=ALU.mult, op1=ALU.subtract))

        def conv_update(g, i, k):
            xc = X[:, ds(i * CH + image_of_step(g) * IMG, CH)]
            dve.wait_ge(conv_mm, i + (NCH * g + 1))
            dve.scalar_tensor_tensor(out=xc, in0=bank(k), scalar=1.0 / (XS * WS), in1=xc,
                                     op0=ALU.mult, op1=ALU.add).then_inc(x_new, 1)

        def conv_stats(g, i, count):
            dve.wait_ge(x_new, count)
            stats_chunk(4 + g, X[:, ds(i * CH + image_of_step(g) * IMG, CH)], i)

        def conv_chunks(g, i0, i1):
            with_stats = g < 8
            start = i0 + 1 if with_stats else i0
            if with_stats:
                conv_update(g, i0, i0 % RING)
            if start < i1:
                with dve.Fori(start, i1) as i:
                    conv_update(g, i, i - i0 // RING * RING)
                    if with_stats:
                        conv_stats(g, i - 1, i + (x_new_at[("c", g, 0)] - 1))
            if with_stats:
                conv_stats(g, i1 - 1, x_new_at[("c", g, i1 - 1)])
                bn_count[0] += i1 - i0

        def xt_low(b, j):
            m = NCH * b + j
            dve.wait_ge(xt_hi, m + 1)
            dve.tensor_tensor(xt_part(b, j, 1), tr_bank(m), xt_part(b, j, 0), ALU.subtract
                              ).then_inc(xt_lo, 1)

        def mlp_chunk(b, i):
            m = NCH * b + i
            xc = X[:, b * IMG + i * CH:b * IMG + (i + 1) * CH]
            dve.wait_ge(ty_mm, m + 1)
            dve.tensor_tensor(xc, bank(TR_BANK + m % 2), xc, ALU.add).then_inc(x_new, 1)
            dve.wait_ge(x_new, x_new_at[("y", b, i)])
            if i == 0:
                dve.wait_ge(*aggregated(8 + b))
            stats_chunk(12 + b, xc, i)
            bn_count[0] += 1

        def split_low(src, dst, landed, high, made, e):
            dve.wait_ge(landed, 16 * e + 16)
            dve.wait_ge(high, e + 1)
            dve.scalar_tensor_tensor(out=dst[:, 1], in0=src[:], scalar=WS, in1=dst[:, 0],
                                     op0=ALU.mult, op1=ALU.subtract).then_inc(made, 1)

        def zero_pads(s):
            dve.memset(XN[s][:, :, :, 0:PITCH:PITCH - 1], 0.0).then_inc(pads_ok[s], 1)

        def zero_halo(s):
            dve.memset(HALO[s][0:ONES, 0:NT:NT - 1], 0.0).then_inc(halo_ok[s], 1)

        def set_ones(s):
            dve.memset(HALO[s][ONES:KH].bitcast(U32), ONES_BITS).then_inc(halo_ok[s], 1)

        def other_work(g, i):
            if g >= 5:
                for b, j in prepared_after(g, i):
                    xt_low(b, j)
            for n in finishing(g, i, 0):
                if n > 3:
                    deviation(n)
            for n in finishing(g, i, 1):
                if n > 2:
                    variance(n)
            if (g, i) == (0, 2):
                input_stats(2, 3, NCH)
            if (g, i) == (0, 5):
                deviation(2)
            if (g, i) == (0, 6):
                variance(2)
            if g in (3, 4) and i == 0:
                build_products(g - 2)
                build_parts(g - 2)
            if (g, i) == (7, 1):
                split_low(W1F, W1S, w1_in, w1_hi, w1_ok, 0)

        for s in range(2):
            zero_pads(s)
            zero_halo(s)
        set_ones(0)
        dve.memset(MSK[:, 3, 0:2], 0.0).then_inc(msk_ok, 1)
        dve.wait_ge(const_ok, MASKS_MADE)
        dve.tensor_reduce(MSK[:, 0], BAND[:].rearrange("p y c r -> p y r c"), AX_X, ALU.add
                          ).then_inc(msk_ok, 1)
        dve.wait_ge(msk_ok, 2)
        dve.tensor_copy(MSK[:, 1:KX], MSK[:, 0:1].broadcast_to([P, KX - 1, KY, R])
                        ).then_inc(msk_ok, 1)
        dve.tensor_reduce(MSK[:, 3, 0:KY:KY - 1], EDGE[:].rearrange("p h s r -> p s r h"),
                          AX_X, ALU.add).then_inc(msk_ok, 1)
        dve.wait_ge(msk_ok, 4)
        dve.memset(MSK[ONES:KH, 3, 0], 1.0).then_inc(msk_ok, 1)
        input_stats(0, 0, FIRST_TILES // TC)
        build_product(0, 0)
        input_stats(0, FIRST_TILES // TC, NCH)
        deviation(0)
        build_product(0, 1)
        variance(0)
        build_product(0, 2)
        build_parts(0)
        input_stats(1, 0, NCH)
        for g in range(8):
            dve.wait_ge(*aggregated(g))
            if g == 0:
                input_stats(2, 0, 2)
                deviation(1)
                input_stats(2, 2, 3)
                variance(1)
            if g == 1:
                input_stats(3, 0, NCH)
                deviation(3)
            stops = statistics_stops(g) | {0, RING - 1, NCH - 1}
            if g == 0:
                stops |= {5}
            if g >= 5:
                stops = set(range(NCH))
            ends = [i + 1 for i in sorted(stops)]
            for i0, i1 in zip([0] + ends, ends):
                conv_chunks(g, i0, i1)
                other_work(g, i1 - 1)
            aggregate(4 + g)

        def hidden(e, p, extra=None, first=False, high=True):
            if not first:
                dve.wait_ge(g2_mm, e * 4 + (2 * p - 2))
            for ft in range(FT):
                a = e * 16 + (p * FT + ft)
                if high:
                    dve.wait_ge(gelu_ok, a + 1)
                    dve.tensor_scalar(HID[p][:, 0, ft], SCR[:, ft % 2], HS, None, ALU.mult
                                      ).then_inc(hid_hi, 1)
                dve.wait_ge(hid_hi, a + 1)
                dve.scalar_tensor_tensor(out=HID[p][:, 1, ft], in0=SCR[:, ft % 2],
                                         scalar=HS, in1=HID[p][:, 0, ft], op0=ALU.mult,
                                         op1=ALU.subtract).then_inc(hid_ok, 1)
                if extra is not None:
                    extra(ft)

        def next_w1(e):
            split_low(W1F, W1S, w1_in, w1_hi, w1_ok, e)

        def w2_parts(e):
            split_low(W2F, W2S, w2_in, w2_hi, w2_ok, e)

        def in_first(ft):
            if ft == 1:
                deviation(11)
            if ft == 3:
                variance(11)
                w2_parts(0)

        hidden(0, 0, in_first, first=True)
        for j in range(NCH):
            xt_low(3, j)
        dve.wait_ge(pre_mm, NB * NCH)
        hidden(0, 1, first=True)
        next_w1(1)
        with dve.Fori(1, NE - 1) as e:
            w2_parts(e)
            for p in range(NPAIR):
                hidden(e, p)
            next_w1(e + 1)

        e = NE - 1
        w2_parts(e)
        hidden(e, 0)
        dve.wait_ge(w1_ok, NE)
        zero_halo(0)
        dve.wait_ge(w2_ok, NE)
        zero_halo(1)

        hidden(e, 1, lambda ft: mlp_chunk(0, ft), high=False)
        aggregate(12)
        deviation(12)
        mlp_chunk(1, 0)
        variance(12)
        dve.wait_ge(g2_mm, 4 * (NE - 1) + 2)
        zero_pads(0)
        for i in range(1, NCH):
            mlp_chunk(1, i)
        aggregate(13)
        dve.wait_ge(g2_mm, 4 * NE)
        zero_pads(1)

        def statistics(g, i):
            for n in finishing(g, i, 0):
                deviation(n)
            for n in finishing(g, i, 1):
                variance(n)

        mlp_chunk(2, 0)
        deviation(13)
        mlp_chunk(2, 1)
        mlp_chunk(2, 2)
        variance(13)
        for i in range(3, 6):
            mlp_chunk(2, i)
        for i in range(NCH):
            if i == RING:
                mlp_chunk(2, 6)
                mlp_chunk(2, 7)
                aggregate(14)
            conv_update(8, i, i % RING)
            if i > 1:
                statistics(8, i)
        for i in range(NCH):
            if i < NCH // 2:
                mlp_chunk(3, 2 * i)
                mlp_chunk(3, 2 * i + 1)
            conv_update(9, i, i % RING)
            if i == NCH // 2 - 1:
                aggregate(15)
            statistics(9, i)
        for g in (10, 11):
            conv_chunks(g, 0, RING)
            conv_chunks(g, RING, NCH)

    @block.tensor
    def _(pe):
        def group_mean(n):
            pe.wait_ge(*aggregated(n))
            if n in (12, 13):
                if n == 12:
                    pe.wait_ge(gelu_ok, NE * NPAIR * FT)
                else:
                    pe.wait_ge(yt_ok, 4 * NE)
            elif n >= 2:
                pe.wait_ge(var_ok, 2 * (n - 1))
            pe.matmul(stat_psum(n, 0), GRP[:], MV[:, n, 0:1], start=True, stop=True
                      ).then_inc(mean_mm, 1)

        def group_variance(n):
            pe.wait_ge(spread_ok, n + 1)
            pe.matmul(stat_psum(n, 1), GRP[:], SM[:, n, 1:2], start=True, stop=True
                      ).then_inc(var_mm, 1)

        def conv_main(g, i, k):
            s, l = g % 2, g // 4
            pe.wait_ge(hi_ok, i + (NCH * g + 1))
            n = 0
            for part, w in ((0, 0), (0, 1), (1, 0)):
                if part == 1:
                    pe.wait_ge(lo_ok, i + (NCH * g + 1))
                for kx in range(KX):
                    rhs = XN[s][:, part, ds(i * TC, TC), kx:kx + NW]
                    pe.matmul(bank(k), CWT[:, l, w, kx], rhs, start=(n == 0), stop=False)
                    n += 1

        def conv_halo(g, i, k):
            s, l = g % 2, g // 4
            if g == 0 and i * TC < HALO_TILES:
                pe.wait_ge(halo_first, 64)
            else:
                pe.wait_ge(halo_in[s], 64 * (g // 2 + 1))
            for w in range(2):
                rhs = HALO[s][0:KH, ds(i * TC, TC), 0:NW]
                mm = pe.matmul(bank(k), CWT[0:KH, l, w, 3], rhs, start=False, stop=(w == 1))
            mm.then_inc(conv_mm, 1)

        def conv_chunk(g, i, k):
            conv_main(g, i, k)
            conv_halo(g, i, k)

        def statistics(g, i):
            for n in finishing(g, i, 0):
                group_mean(n)
            for n in finishing(g, i, 1):
                group_variance(n)

        def before_step(g):
            if g % 4 == 0:
                pe.wait_ge(build_ok[g // 4], BUILD_STEPS)
            pe.wait_ge(pads_ok[g % 2], 1 if g < 8 else 2)
            pe.wait_ge(halo_ok[g % 2], 2 if g < 8 else 4)

        def conv_chunks(g, i0, i1):
            before = x_new_at[("c", g + (i0 - RING) // NCH, (i0 - RING) % NCH)]
            with pe.Fori(i0, i1) as i:
                pe.wait_ge(x_new, i + (before - i0))
                conv_chunk(g, i, i - i0 // RING * RING)

        def pre_transposes(b, j):
            m = NCH * b + j
            pe.wait_ge(pre_ok, m + 1)
            if m == 0:
                pe.wait_ge(build_ok[2], BUILD_STEPS)
            if m == 1:
                pe.wait_ge(bt_ok, 1)
            if m >= 2:
                pe.wait_ge(xt_lo, m - 1)
            to = bank(TR_BANK + m % 2)
            for h in range(DH):
                for t in range(TC):
                    mm = pe.transpose(to[:, (h * TC + t) * P:(h * TC + t + 1) * P],
                                      pre(b, j)[:, t * NW + h * P:t * NW + (h + 1) * P], IDF[:])
            mm.then_inc(pre_mm, 1)

        def result_transposes(b, i):
            m = NCH * b + i
            if m < 2:
                pe.wait_ge(xt_lo, NB * NCH)
                pe.wait_ge(yt_ok, 4 * (NE - 1) + 2)
            else:
                pe.wait_ge(x_new, x_new_at[("y", (m - 2) // NCH, (m - 2) % NCH)])
            if b >= 2:
                pe.wait_ge(yt_ok, 4 * NE)
            to = bank(TR_BANK + m % 2)
            for t in range(TC):
                for h in range(DH):
                    tt = (b % 2) * NT + i * TC + t
                    mm = pe.transpose(to[:, t * NW + h * P:t * NW + (h + 1) * P],
                                      YT[:, b // 2, h, tt], IDF[:])
            mm.then_inc(ty_mm, 1)

        def hidden(e, p, between=None):
            for ft in range(FT):
                a = e * 16 + (p * FT + ft)
                if isinstance(e, int) and a < RING:
                    pe.wait_ge(x_new, x_new_at[("c", 7, NCH - RING + a)])
                else:
                    pe.wait_ge(gelu_ok, a - (RING - 1))
                if ft == 0:
                    pe.wait_ge(w1_ok, e + 1)
                    if isinstance(e, int) and e == 0:
                        pe.wait_ge(xt_lo, 2 * NCH * (p + 1))
                n = 0
                for h in range(DH):
                    for part, w in ((0, 0), (1, 0), (0, 1)):
                        mm = pe.matmul(
                            bank(ft % RING),
                            W1S[:, w, h * NF + ft * P:h * NF + (ft + 1) * P],
                            XT[:, p, h, :, e, part], start=(n == 0),
                            stop=(n == 3 * DH - 1))
                        n += 1
                mm.then_inc(g1_mm, 1)
                if between is not None:
                    between(ft)

        def output(e, p, h, between=None):
            k = p * DH + h
            if isinstance(e, int) and 4 * e + k < 2:
                pe.wait_ge(var_ok, 2 * 12)
            else:
                pe.wait_ge(yt_ok, e * 4 + (k - 1))
            for ft in range(FT):
                if h == 0:
                    pe.wait_ge(hid_ok, e * 16 + (p * FT + ft + 1))
                if ft == 0 and k == 0:
                    pe.wait_ge(w2_ok, e + 1)
                for part, w in ((0, 0), (1, 0), (0, 1)):
                    mm = pe.matmul(bank(G2_BANK + h),
                                   W2S[:, w, ft * NW + h * P:ft * NW + (h + 1) * P],
                                   HID[p][:, part, ft],
                                   start=(ft == 0 and part == 0 and w == 0),
                                   stop=(ft == FT - 1 and w == 1))
                if between is not None:
                    if ft == FT - 1:
                        mm.then_inc(g2_mm, 1)
                    between(ft)
            if between is None:
                mm.then_inc(g2_mm, 1)

        def expert(e):
            for p in range(NPAIR):
                hidden(e, p)
            for p in range(NPAIR):
                for h in range(DH):
                    output(e, p, h)

        pe.wait_ge(const_ok, SELW_MADE)
        pe.wait_ge(cw_in, 32)
        for k in range(4):
            pe.matmul(TAPS[:, k].rearrange("p l y o -> p (l y o)"), SELW[:, k],
                      WK[:].rearrange("k l y o -> k (l y o)"), start=True, stop=True
                      ).then_inc(taps_mm, 1)
        pe.wait_ge(const_ok, CONSTS_MADE)
        pe.wait_ge(bb_in, 32)
        nb = (FT + DH) * NE
        pe.transpose(bank(TR_BANK + 1)[:, 0:nb], BB[:], IDF[0:nb, 0:nb]).then_inc(bt_mm, 1)
        group_mean(0)
        group_variance(0)
        for _ in range(WARM_UP):
            pe.matmul(PS[:, 0:P], GRP[:], IDF[:], start=True, stop=True)
        for g in range(2):
            before_step(g)
            for part, i in LATE_HALO:
                if part == "main":
                    if i >= RING or g > 0:
                        pe.wait_ge(x_new, x_new_at[("c", g + (i - RING) // NCH, (i - RING) % NCH)])
                    conv_main(g, i, i % RING)
                    if i < RING:
                        statistics(g, i)
                else:
                    conv_halo(g, i, i % RING)
                    if i >= RING:
                        statistics(g, i)
        for g in range(2, 8):
            before_step(g)
            if g < 5:
                stops = sorted({i + 1 for i in statistics_stops(g)} | {RING, NCH})
                for i0, i1 in zip([0] + stops, stops):
                    conv_chunks(g, i0, i1)
                    statistics(g, i1 - 1)
            else:
                for i in range(NCH):
                    pe.wait_ge(x_new, x_new_at[("c", g + (i - RING) // NCH, (i - RING) % NCH)])
                    conv_chunk(g, i, i % RING)
                    statistics(g, i)
                    for b, j in prepared_after(g, i):
                        pre_transposes(b, j)

        def in_first_hidden(ft):
            if ft == 1:
                group_mean(11)
            if ft == 3:
                group_variance(11)

        def in_first_output(ft):
            steps = [2, 4, 5, 7, 9, 10, 12, 13]
            if h * FT + ft in steps:
                pre_transposes(3, steps.index(h * FT + ft))

        hidden(0, 0, in_first_hidden)
        for h in range(DH):
            output(0, 0, h, in_first_output)
        hidden(0, 1)
        for h in range(DH):
            output(0, 1, h)
        with pe.Fori(1, NE - 1) as e:
            expert(e)
        e = NE - 1
        hidden(e, 0)
        for h in range(DH):
            output(e, 0, h)

        def in_output_0(ft):
            if ft == 5:
                group_mean(12)
                result_transposes(1, 0)
            if ft == 7:
                group_variance(12)
                result_transposes(1, 1)

        def in_output_1(ft):
            if ft < 7 and ft != 3:
                result_transposes(1, 2 + (ft if ft < 3 else ft - 1))

        hidden(e, 1, lambda ft: result_transposes(0, ft))
        output(e, 1, 0, in_output_0)
        output(e, 1, 1, in_output_1)

        before_step(8)
        for i in range(RING):
            if i == 0:
                pe.wait_ge(gelu_ok, NE * NPAIR * FT)
                pe.wait_ge(var_ok, 2 * 13)
            conv_main(8, i, i)
            if i < 3:
                result_transposes(2, 2 * i)
                result_transposes(2, 2 * i + 1)
            statistics(8, i)
        for i in range(RING):
            conv_halo(8, i, i)
        for i in range(RING, NCH):
            pe.wait_ge(x_new, x_new_at[("c", 8, i - RING)])
            conv_chunk(8, i, i - RING)
            if i == RING:
                result_transposes(2, 6)
                result_transposes(2, 7)
            statistics(8, i)
        before_step(9)
        for i in range(NCH):
            if i < NCH // 2:
                result_transposes(3, 2 * i)
                result_transposes(3, 2 * i + 1)
            pe.wait_ge(x_new, x_new_at[("c", 9 + (i - RING) // NCH, (i - RING) % NCH)])
            conv_chunk(9, i, i % RING)
            statistics(9, i)
        for g in (10, 11):
            before_step(g)
            conv_chunks(g, 0, RING)
            conv_chunks(g, RING, NCH)

    ctx.close()


CONVS = ("L0", "L1", "L3")
DENSE = ("L2_conv_w1", "L2_conv_b1", "L2_conv_w2", "L2_conv_b2")


def kernel(**inputs):
    import concourse.bacc as bacc
    import numpy as np
    from concourse.bass_utils import run_bass_kernel_spmd

    nc = bacc.Bacc("TRN2", target_bir_lowering=False, num_devices=1)
    arrays = {name: np.asarray(inputs[name]) for name in ("x",) + DENSE}
    weights = np.stack([np.asarray(inputs[f"{l}_conv_weight"]) for l in CONVS])
    arrays["conv_weights"] = weights.transpose(2, 4, 0, 3, 1)
    arrays["conv_biases"] = np.stack([np.asarray(inputs[f"{l}_conv_bias"]) for l in CONVS])
    arrays = {name: np.ascontiguousarray(a) for name, a in arrays.items()}
    t = {name: nc.dram_tensor(name, a.shape, F32, kind="ExternalInput").ap()
         for name, a in arrays.items()}
    out = nc.dram_tensor("out", (NB, NC, NH, NW), F32, kind="ExternalOutput").ap()
    bass_program(nc, t["x"], t["conv_weights"], t["conv_biases"], *(t[n] for n in DENSE), out)
    return run_bass_kernel_spmd(nc, [arrays], core_ids=[0]).results[0]["out"]
```
